# Optimizing a Trainium2 kernel written in Bass

```python
import numpy as np
import jax
import jax.numpy as jnp

def _softmax(x, axis=-1):
    return jax.nn.softmax(x, axis=axis)

def _gelu(x):
    return jax.nn.gelu(x, approximate=True)

def _silu(x):
    return jax.nn.silu(x)

def _sigmoid(x):
    return jax.nn.sigmoid(x)

def _layernorm(x, axis=-1, eps=1e-05):
    m = jnp.mean(x, axis=axis, keepdims=True)
    v = jnp.var(x, axis=axis, keepdims=True)
    return (x - m) / jnp.sqrt(v + eps)

def _scatter_add(tgt, idx, src, axis=0):
    return tgt.at[idx].add(src)

def _segment_sum(src, seg, n):
    return jax.ops.segment_sum(src, seg, n)
kernel_name = 'mk_hybrid_d1_jaxref_r8_27d63e'

def setup_inputs(seed: int=0):
    np.random.seed(seed)
    _w = jnp.asarray

    def _L0_attn_a_setup():
        import jax, jax.numpy as jnp
        import numpy as np
        DIM = 128
        NUM_HEADS = 16
        HD = DIM // NUM_HEADS
        ROPE_DIM = 64
        ROPE_BASE = 10000.0

        def _apply_rope(t):
            D = t.shape[-1]
            N = t.shape[2]
            pos = jnp.arange(N, dtype=t.dtype)
            inv = 1.0 / ROPE_BASE ** (jnp.arange(0, D, 2, dtype=t.dtype) / D)
            freqs = pos[:, None] * inv[None, :]
            cos = jnp.cos(freqs)[None, None]
            sin = jnp.sin(freqs)[None, None]
            e = t[..., 0::2]
            o = t[..., 1::2]
            eo = e * cos - o * sin
            oo = e * sin + o * cos
            return jnp.stack([eo, oo], axis=-1).reshape(t.shape)
        key = jax.random.key(seed)
        ks = jax.random.split(key, 5)
        B, N = (2, 256)
        s = 0.02
        return {'x': jax.random.normal(ks[0], (B, N, DIM), dtype=jnp.float32), 'qkv_w': jax.random.normal(ks[1], (3 * DIM, DIM), dtype=jnp.float32) * s, 'qkv_b': jax.random.normal(ks[2], (3 * DIM,), dtype=jnp.float32) * s, 'proj_w': jax.random.normal(ks[3], (DIM, DIM), dtype=jnp.float32) * s, 'proj_b': jax.random.normal(ks[4], (DIM,), dtype=jnp.float32) * s}
    _L0_attn_a_in = _L0_attn_a_setup()

    def _L0_attn_b_setup():
        import jax, jax.numpy as jnp
        import numpy as np
        HEADS = 16
        key = jax.random.key(seed)
        k1, k2, k3 = jax.random.split(key, 3)
        B, N, C = (4, 512, 128)
        x = jax.random.normal(k1, (B, N, C), dtype=jnp.float32)
        w_qkv = jax.random.normal(k2, (3 * C, C), dtype=jnp.float32) * C ** (-0.5)
        w_proj = jax.random.normal(k3, (C, C), dtype=jnp.float32) * C ** (-0.5)
        b_proj = jnp.zeros((C,), dtype=jnp.float32)
        return {'x': x, 'w_qkv': w_qkv, 'w_proj': w_proj, 'b_proj': b_proj}
    _L0_attn_b_in = _L0_attn_b_setup()

    def _L0_ffn_setup():
        import jax, jax.numpy as jnp
        import numpy as np
        DIM = 128

        def _reference_tuple_inner(x, W_r, W_k, W_v, mu_r, mu_k):
            B, T, C = x.shape
            x_prev = jnp.concatenate([jnp.zeros((B, 1, C), x.dtype), x[:, :-1, :]], axis=1)
            xr = mu_r * x + (1.0 - mu_r) * x_prev
            xk = mu_k * x + (1.0 - mu_k) * x_prev
            r = jax.nn.sigmoid(jnp.einsum('btc,dc->btd', xr, W_r))
            k = jnp.einsum('btc,dc->btd', xk, W_k)
            k_act = jnp.square(jax.nn.relu(k))
            out = r * jnp.einsum('btc,dc->btd', k_act, W_v)
            new_state = x[:, -1, :]
            return (out, new_state)
        key = jax.random.key(seed)
        ks = jax.random.split(key, 6)
        B, T, C = (8, 256, DIM)
        x = jax.random.normal(ks[0], (B, T, C), dtype=jnp.float32)
        s = 1.0 / np.sqrt(C)
        W_r = jax.random.uniform(ks[1], (C, C), jnp.float32, -s, s)
        W_k = jax.random.uniform(ks[2], (C, C), jnp.float32, -s, s)
        W_v = jax.random.uniform(ks[3], (C, C), jnp.float32, -s, s)
        mu_r = jax.random.uniform(ks[4], (C,), jnp.float32)
        mu_k = jax.random.uniform(ks[5], (C,), jnp.float32)
        return {'x': x, 'W_r': W_r, 'W_k': W_k, 'W_v': W_v, 'mu_r': mu_r, 'mu_k': mu_k}
    _L0_ffn_in = _L0_ffn_setup()
    _d = {'L0_attn_a_x': _L0_attn_a_in['x'], 'L0_attn_a_qkv_w': _L0_attn_a_in['qkv_w'], 'L0_attn_a_qkv_b': _L0_attn_a_in['qkv_b'], 'L0_attn_a_proj_w': _L0_attn_a_in['proj_w'], 'L0_attn_a_proj_b': _L0_attn_a_in['proj_b'], 'L0_attn_b_w_qkv': _L0_attn_b_in['w_qkv'], 'L0_attn_b_w_proj': _L0_attn_b_in['w_proj'], 'L0_attn_b_b_proj': _L0_attn_b_in['b_proj'], 'L0_ffn_W_r': _L0_ffn_in['W_r'], 'L0_ffn_W_k': _L0_ffn_in['W_k'], 'L0_ffn_W_v': _L0_ffn_in['W_v'], 'L0_ffn_mu_r': _L0_ffn_in['mu_r'], 'L0_ffn_mu_k': _L0_ffn_in['mu_k']}
    _x0 = _d['L0_attn_a_x']
    _d['L0_attn_a_x'] = jax.random.normal(jax.random.fold_in(jax.random.key(seed), 1), (1, 2048, 128), dtype=_x0.dtype)
    del _x0
    return _d

def reference(L0_attn_a_x, L0_attn_a_qkv_w, L0_attn_a_qkv_b, L0_attn_a_proj_w, L0_attn_a_proj_b, L0_attn_b_w_qkv, L0_attn_b_w_proj, L0_attn_b_b_proj, L0_ffn_W_r, L0_ffn_W_k, L0_ffn_W_v, L0_ffn_mu_r, L0_ffn_mu_k):

    def _L0_attn_a_ref(x, qkv_w, qkv_b, proj_w, proj_b):
        import jax, jax.numpy as jnp
        import numpy as np
        DIM = 128
        NUM_HEADS = 16
        HD = DIM // NUM_HEADS
        ROPE_DIM = 64
        ROPE_BASE = 10000.0

        def _apply_rope(t):
            D = t.shape[-1]
            N = t.shape[2]
            pos = jnp.arange(N, dtype=t.dtype)
            inv = 1.0 / ROPE_BASE ** (jnp.arange(0, D, 2, dtype=t.dtype) / D)
            freqs = pos[:, None] * inv[None, :]
            cos = jnp.cos(freqs)[None, None]
            sin = jnp.sin(freqs)[None, None]
            e = t[..., 0::2]
            o = t[..., 1::2]
            eo = e * cos - o * sin
            oo = e * sin + o * cos
            return jnp.stack([eo, oo], axis=-1).reshape(t.shape)
        B, N, C = x.shape
        H, D = (NUM_HEADS, HD)
        scale = D ** (-0.5)
        qkv = x @ qkv_w.T + qkv_b
        qkv = qkv.reshape(B, N, 3, H, D).transpose(2, 0, 3, 1, 4)
        q, k, v = (qkv[0], qkv[1], qkv[2])
        q = jnp.concatenate([_apply_rope(q[..., :ROPE_DIM]), q[..., ROPE_DIM:]], axis=-1)
        k = jnp.concatenate([_apply_rope(k[..., :ROPE_DIM]), k[..., ROPE_DIM:]], axis=-1)
        attn = jnp.einsum('bhnd,bhmd->bhnm', q, k) * scale
        attn = jax.nn.softmax(attn, axis=-1)
        out = jnp.einsum('bhnm,bhmd->bhnd', attn, v)
        out = out.transpose(0, 2, 1, 3).reshape(B, N, C)
        return out @ proj_w.T + proj_b

    def _L0_attn_b_ref(x, w_qkv, w_proj, b_proj):
        import jax, jax.numpy as jnp
        import numpy as np
        HEADS = 16
        B, N, C = x.shape
        H = HEADS
        D = C // H
        qkv = x @ w_qkv.T
        q, k, v = jnp.split(qkv, 3, axis=-1)

        def to_bhdn(t):
            return t.reshape(B, N, H, D).transpose(0, 2, 3, 1)
        q = jax.nn.relu(to_bhdn(q))
        k = jax.nn.relu(to_bhdn(k))
        v = to_bhdn(v)
        eps = jnp.finfo(q.dtype).eps
        ksum = k.sum(axis=-1)
        z = 1.0 / (jnp.einsum('bhd,bhdn->bhn', ksum, q) + eps)
        context = jnp.einsum('bhdn,bhen->bhde', v, k)
        out = jnp.einsum('bhde,bhen->bhdn', context, q)
        out = out * z[:, :, None, :]
        out = out.transpose(0, 3, 1, 2).reshape(B, N, C)
        return out @ w_proj.T + b_proj

    def _L0_ffn_ref(x, W_r, W_k, W_v, mu_r, mu_k):
        import jax, jax.numpy as jnp
        import numpy as np
        DIM = 128

        def _reference_tuple_inner(x, W_r, W_k, W_v, mu_r, mu_k):
            B, T, C = x.shape
            x_prev = jnp.concatenate([jnp.zeros((B, 1, C), x.dtype), x[:, :-1, :]], axis=1)
            xr = mu_r * x + (1.0 - mu_r) * x_prev
            xk = mu_k * x + (1.0 - mu_k) * x_prev
            r = jax.nn.sigmoid(jnp.einsum('btc,dc->btd', xr, W_r))
            k = jnp.einsum('btc,dc->btd', xk, W_k)
            k_act = jnp.square(jax.nn.relu(k))
            out = r * jnp.einsum('btc,dc->btd', k_act, W_v)
            new_state = x[:, -1, :]
            return (out, new_state)
        return _reference_tuple_inner(x, W_r, W_k, W_v, mu_r, mu_k)[0]
    x = L0_attn_a_x
    x = x + _L0_attn_a_ref(_layernorm(x, axis=-1), L0_attn_a_qkv_w, L0_attn_a_qkv_b, L0_attn_a_proj_w, L0_attn_a_proj_b)
    x = x + _L0_ffn_ref(_layernorm(x, axis=-1), L0_ffn_W_r, L0_ffn_W_k, L0_ffn_W_v, L0_ffn_mu_r, L0_ffn_mu_k)
    x = x + _L0_attn_b_ref(_layernorm(x, axis=-1), L0_attn_b_w_qkv, L0_attn_b_w_proj, L0_attn_b_b_proj)
    x = x + _L0_ffn_ref(_layernorm(x, axis=-1), L0_ffn_W_r, L0_ffn_W_k, L0_ffn_W_v, L0_ffn_mu_r, L0_ffn_mu_k)
    return x

_drawn_inputs = setup_inputs


def setup_inputs(seed=0):
    import zlib

    import numpy as np

    out = dict(_drawn_inputs(seed))
    spreads = {'L0_attn_b_b_proj': (0.0, 0.1)}
    factors = {'L0_attn_a_qkv_w': 8.0,
     'L0_attn_a_qkv_b': 7.989,
     'L0_attn_a_proj_w': 8.0,
     'L0_ffn_mu_r': 11.432,
     'L0_attn_a_proj_b': 7.892}
    for name, (base, spread) in spreads.items():
        noise = np.random.default_rng([zlib.crc32(name.encode()), seed]).standard_normal(out[name].shape)
        drawn = base * np.exp(spread * noise) if base else spread * noise
        out[name] = jnp.asarray(drawn.astype(out[name].dtype))
    for name, factor in factors.items():
        out[name] = (out[name] * factor).astype(out[name].dtype)
    return out
```

```python
from contextlib import ExitStack

import concourse.bass as bass
from concourse import mybir

ALU = mybir.AluOpType
ACT = mybir.ActivationFunctionType
AX = mybir.AxisListType
F32 = mybir.dt.float32
BF16 = mybir.dt.bfloat16

P = 128
N = 2048
C = 128
H = 16
D = C // H
NT = N // P
CHUNKS = 4
TPC = NT // CHUNKS
CW = N // CHUNKS
QUADS = 4
HQ = H // QUADS
UNITS = CHUNKS * QUADS
STEPS = NT
LN_EPS = 1e-5
Z_EPS = 2.0 ** -23
SCALE = float(D) ** -0.5

SL = 64
S_MAX = 32
S_C = 40

SCORE_BANKS = 3
PROBS = 8
LEAD = STEPS + 3

B_PAIR = 0
B_RING = 4
B_OUT = 7

W_COLS = {}
for _name, _n in (("qkv", 3 * C), ("qkv_b", 3 * C), ("proj", C), ("proj_b", C), ("lin_qkv", 3 * C), ("lin_proj", C),
                  ("lin_proj_b", C), ("r", C), ("k", C), ("v", C), ("mu", 2)):
    W_COLS[_name] = (sum(n for _, n in W_COLS.values()), _n)
W_TOTAL = sum(n for _, n in W_COLS.values())
W_FIRST = 6 * C
K_COS, K_SIN, K_IDENT, K_BLOCK, K_TOTAL = 0, 64, 128, 256, 384


def ring_places(first, last):
    places, at = {}, 0
    for n in range(first, last + 1):
        for kt in range(STEPS):
            if kt == 4 and n % QUADS == 0 and n > 0:
                for i in range(3):
                    places[("att", n, i)] = at
                    at += 1
            if kt == 8 and n + 2 < UNITS:
                places[("queries", n + 2)] = at
                at += 1
            for h in range(HQ):
                places[("scores", n, kt, h)] = at
                at += 1
            if kt == 15 and n + 1 < UNITS:
                places[("stack", n + 1)] = at
                at += 1
    return places, at


def build(nc, x_in, w_in, k_in, out):
    ctx = ExitStack()
    with ctx:
        def sb(name, shape, dt):
            return ctx.enter_context(nc.sbuf_tensor(name, shape, dt))

        def sem(name):
            return ctx.enter_context(nc.semaphore(name))

        ps = ctx.enter_context(nc.psum_tensor("ps", [P, 8, 512], F32))
        w = sb("w", [P, W_TOTAL], F32)
        kc = sb("kc", [P, K_TOTAL], F32)
        identb = sb("identb", [P, P], BF16)
        x = sb("x", [P, NT, C], F32)
        stats = sb("stats", [P, TPC, 6], F32)
        mv = sb("mv", [P, 2, TPC, 2], F32)
        ve = sb("ve", [P, TPC], F32)
        neghalf = sb("neghalf", [P, TPC], F32)
        rstd = sb("rstd", [P, 2, TPC], F32)
        xn = sb("xn", [P, 2, TPC, C], F32)
        ht0 = sb("ht0", [P, N + 1], F32)
        kb = sb("kb", [P, H // 2, N], BF16)
        vt = sb("vt", [P, NT, H, 32], F32)
        qa = sb("qa", [P, 2, HQ, CW], BF16)
        qb = sb("qb", [P, 2, 2, CW], BF16)
        mpart = sb("mpart", [P, 2, TPC, HQ, TPC], F32)
        negm = sb("negm", [P, TPC, HQ], F32)
        rsum = sb("rsum", [P, TPC, HQ], F32)
        qn_raw = sb("qn_raw", [P, NT * H * SL // 2], F32)
        kn_raw = sb("kn_raw", [P, NT * H * SL // 2], F32)
        first = sb("first", [P, 3, TPC, 2 * C], F32)

        qn = qn_raw[:, :].bitcast(BF16).rearrange("p (t h s) -> p t h s", t=NT, h=H)
        kn = kn_raw[:, :].bitcast(BF16).rearrange("p (t h s) -> p t h s", t=NT, h=H)
        kn_rows = kn_raw[:, :].bitcast(BF16).rearrange("p (t s) -> p t s", t=NT)
        qn_rows = qn_raw[:, :].bitcast(BF16).rearrange("p (t s) -> p t s", t=NT)
        qk, rot, tmp = first[:, 0], first[:, 1], first[:, 2]
        probs = kn_raw[:, 0:PROBS * 512].rearrange("p (b n) -> p b n", b=PROBS)
        at = PROBS * 512
        ot = kn_raw[:, at:at + 2 * 512].rearrange("p (b n) -> p b n", b=2)
        at += 2 * 512
        attn = kn_raw[:, at:at + CW].rearrange("p (t c) -> p t c", t=TPC)
        at += CW
        attT = kn_raw[:, at:at + 512]

        def wcol(name, a=0, b=None):
            at, n = W_COLS[name]
            return w[:, at + a:at + (n if b is None else b)]

        ident = kc[:, K_IDENT:K_IDENT + P]
        cos = kc[:, K_COS:K_COS + 64].rearrange("p (t i) -> p t i", t=NT)
        sin = kc[:, K_SIN:K_SIN + 64].rearrange("p (t i) -> p t i", t=NT)
        block_mask = kc[:, K_BLOCK:K_BLOCK + P]

        ht1 = qn_raw[:, 0:N + 1]
        qt = qn_raw[:, N + 4:2 * N + 4]
        o = 2 * N + 4
        sg = qn_raw[:, o:o + 1024].rearrange("p (b n) -> p b n", b=2)
        kr = qn_raw[:, o + 1024:o + 1536]
        ks = qn_raw[:, o + 1536:o + 2560].rearrange("p (b n) -> p b n", b=2)
        vs = qn_raw[:, o + 2560:o + 3072]
        kn3 = kn_raw[:, 0:1024].rearrange("p (b t c) -> p b t c", b=2, t=TPC)
        vn3 = kn_raw[:, 1024:1024 + 2 * TPC * 132].rearrange("p (b t c) -> p b t c", b=2, t=TPC)
        at3 = kn_raw[:, 2112:3136].rearrange("p (b t c) -> p b t c", b=2, t=TPC)
        att3 = kn_raw[:, 3136:4160].rearrange("p (b n) -> p b n", b=2)
        zz = kn_raw[:, 4160:4160 + 2 * TPC * H].rearrange("p (a t h) -> p a t h", a=2, t=TPC)
        ctxm = kn_raw[:, 4300:4300 + C + H]
        ksum = kn_raw[:, 4450:4451]
        wmix = first[:, 0:1].rearrange("p a t c -> p (a t c)")[:, 0:4 * C].rearrange("p (m c) -> p m c", m=4)
        onem = first[:, 0, 2, 0:2]

        x_in_s = [sem(f"x_loaded{i}") for i in range(CHUNKS)]
        w1_s, w2_s, k_s = sem("first_weights_loaded"), sem("other_weights_loaded"), sem("constants_loaded")
        identb_s = sem("identb_ready")
        pads_s = sem("pads_ready")
        half_s = sem("neghalf_ready")
        stats_s = sem("ln_stats_ready")
        ve_s = sem("pool_chain")
        rstd_s = sem("rstd_ready")
        xn_s = sem("xn_ready")
        xt_s = sem("xn_turned")
        ht_s = sem("ht_ready")
        qkv_s = sem("qkv_ready")
        qkv_used = sem("qkv_used")
        split_s = sem("split_ready")
        dups_s = sem("dups_ready")
        turns_begun = sem("turns_begun")
        kt_s = sem("keys_turned")
        kt_used = sem("keys_stored")
        chain = sem("dve_chain")
        pair_s = sem("pair_ready")
        pair_used = sem("pair_used")
        max_s = sem("max_ready")
        ring_s = sem("ring_ready")
        ring_used = sem("ring_used")
        pv_s = sem("sums_step_done")
        ot_s = sem("sums_stored")
        on_s = sem("sums_turned")
        attn_s = sem("attn_ready")
        proj_s = sem("proj_ready")
        x1_s = sem("x1_ready")
        mix_s = sem("mixed_weights_ready")
        r_s, kk_s, v_s = sem("r_ready"), sem("k_ready"), sem("v_ready")
        sg_s, kr_s, ks_s = sem("sigmoid_ready"), sem("relu_ready"), sem("square_ready")
        xf_s = sem("ffn_added")
        q3_s, kv3_s = sem("lin_q_ready"), sem("lin_kv_ready")
        q3a_s, kv3a_s = sem("lin_q_stored"), sem("lin_kv_stored")
        ctx_s = sem("context_ready")
        ctxm_s = sem("context_masked")
        lo_s = sem("lin_out_ready")
        ln_s = sem("lin_out_scaled")
        lt_s = sem("lin_out_turned")
        lta_s = sem("lin_out_stored")
        lp_s = sem("lin_proj_ready")
        lx_s = sem("lin_added")
        out_s = sem("out_written")

        block = ctx.enter_context(nc.Block())

        head_items, head_n = ring_places(0, 0)
        body_items, body_n = ring_places(1, QUADS)
        tail_items, _ = ring_places(3 * QUADS + 1, UNITS - 1)
        RING0 = 3
        assert (RING0 + head_n) % SCORE_BANKS == 0 and body_n % SCORE_BANKS == 0

        class Part:

            def __init__(self, first, last, items, start, c=0, per_c=0):
                self.first, self.last, self.items, self.start, self.c, self.per = first, last, items, start, c, per_c

            def unit(self, n, times=1, plus=0):
                if self.per:
                    return self.c * (QUADS * times) + (n * times + plus)
                return n * times + plus

            def ring(self, key, plus=1):
                v = self.start + self.items[key] + plus
                return self.c * self.per + v if self.per else v

            def bank(self, key):
                return B_RING + (self.start + self.items[key]) % SCORE_BANKS

            def a_step(self, n, kt):
                s = n * STEPS + kt + LEAD
                if not self.per and s >= UNITS * STEPS:
                    return None
                return s // STEPS, s % STEPS

            def more(self, n, k):
                return bool(self.per) or n + k < UNITS

            def chunk_tile(self, n, t):
                if self.per:
                    return self.c * TPC + (TPC * (n // QUADS) + t)
                return TPC * (n // QUADS) + t

        def attention(eng, step):
            for n in range(0, 1):
                for kt in range(STEPS):
                    step(Part(0, 0, head_items, RING0), n, kt)
            with eng.Fori(0, CHUNKS - 1) as c:
                part = Part(1, QUADS, body_items, RING0 + head_n, c, body_n)
                for n in range(1, QUADS + 1):
                    for kt in range(STEPS):
                        step(part, n, kt)
            start = RING0 + head_n + (CHUNKS - 1) * body_n
            part = Part(3 * QUADS + 1, UNITS - 1, tail_items, start)
            for n in range(3 * QUADS + 1, UNITS):
                for kt in range(STEPS):
                    step(part, n, kt)
            return part

        def before():
            return Part(0, 0, {("queries", 0): 0, ("queries", 1): 1, ("stack", 0): 2}, 0)

        @block.sync
        def _(sp):
            xv = x_in.rearrange("(t p) c -> p t c", p=P)
            ov = out.rearrange("(t p) c -> p t c", p=P)
            sp.dma_start(x[:, 0:TPC, :], xv[:, 0:TPC, :]).then_inc(x_in_s[0], 16)
            sp.dma_start(kc[:, :], k_in).then_inc(k_s, 16)
            sp.dma_start(w[:, 0:W_FIRST], w_in[:, 0:W_FIRST]).then_inc(w1_s, 16)
            for i in range(1, CHUNKS):
                sp.dma_start(x[:, i * TPC:(i + 1) * TPC, :], xv[:, i * TPC:(i + 1) * TPC, :]).then_inc(x_in_s[i], 16)
            sp.dma_start(w[:, W_FIRST:], w_in[:, W_FIRST:]).then_inc(w2_s, 16)
            for i in range(CHUNKS):
                sp.wait_ge(xf_s, CHUNKS + i + 1)
                sp.dma_start(ov[:, i * TPC:(i + 1) * TPC, :], x[:, i * TPC:(i + 1) * TPC, :]).then_inc(out_s, 16)
            sp.wait_ge(out_s, 16 * CHUNKS)

        @block.gpsimd
        def _(pool):
            pool.memset(neghalf[:, :], -0.5).then_inc(half_s, 1)
            for raw in (qn_raw, kn_raw):
                words = raw[:, :].rearrange("p (g s) -> p g s", s=SL // 2)
                pool.memset(words[:, :, S_MAX // 2:S_C // 2], 0.0)
                last = pool.memset(words[:, :, (S_C + 16) // 2:], 0.0)
            last.then_inc(ve_s, 1)
            pool.wait_ge(ve_s, 1)
            pool.memset(kn_raw[:, :].bitcast(BF16).rearrange("p (g s) -> p g s", s=SL)[:, :, S_MAX:S_MAX + 2],
                        1.0).then_inc(pads_s, 1)

            def root(q, links):
                pool.wait_ge(stats_s, q + 1)
                if q >= 1:
                    pool.wait_ge(rstd_s, q)
                pool.tensor_scalar(ve[:, :], mv[:, q % 2, :, 1], LN_EPS, None, ALU.add).then_inc(ve_s, 1)
                pool.wait_ge(ve_s, links)
                pool.tensor_tensor(rstd[:, q % 2, :], ve[:, :], neghalf[:, :], ALU.pow).then_inc(rstd_s, 1)

            pool.wait_ge(half_s, 1)
            root(0, 2)
            pool.memset(vt[:, 0:TPC, :, D:], 0.0)
            pool.memset(qa[:, 0, :, :].bitcast(F32), 0.0)
            root(1, 3)
            pool.memset(vt[:, TPC:2 * TPC, :, D:], 0.0)
            pool.memset(qa[:, 1, :, :].bitcast(F32), 0.0)
            root(2, 4)
            pool.memset(vt[:, 2 * TPC:3 * TPC, :, D:], 0.0)
            root(3, 5)
            pool.memset(vt[:, 3 * TPC:, :, D:], 0.0).then_inc(ve_s, 1)
            pool.wait_ge(ve_s, 6)
            pool.memset(vt[:, :, :, D:D + 1], 1.0).then_inc(pads_s, 1)
            for q in range(CHUNKS, 4 * CHUNKS):
                root(q, q + 3)

        @block.scalar
        def _(act):
            def store_ht(q, dst):
                act.wait_ge(xt_s, q + 1)
                act.activation(dst, ps[:, B_OUT, :], ACT.Copy).then_inc(ht_s, 1)

            def repeats(i):
                act.wait_ge(split_s, i + 1)
                t = slice(i * TPC, (i + 1) * TPC)
                q, k = qn[:, t, :, :], kn[:, t, :, :]
                for z, to, of in ((q, 8, 0), (q, 24, 16), (q, S_C, 0), (k, 16, 0), (k, 24, 8), (k, S_C + 8, 0)):
                    last = act.activation(z[:, :, :, to:to + D], z[:, :, :, of:of + D], ACT.Copy)
                last.then_inc(dups_s, 1)

            def store_keys(i):
                for j in range(4):
                    item = 4 * i + j
                    act.wait_ge(kt_s, item + 1)
                    src = ps[:, B_RING + item % SCORE_BANKS, :].bitcast(BF16).rearrange("p (a n) -> p a n", a=2)
                    cols = slice(i * CW, (i + 1) * CW)
                    act.activation(kb[:, 2 * j:2 * j + 2, cols], src, ACT.Copy).then_inc(kt_used, 1)

            for i in range(CHUNKS):
                store_ht(i, ht0[:, 1 + i * CW:1 + (i + 1) * CW])
                if i >= 1:
                    repeats(i - 1)
                if i >= 2:
                    store_keys(i - 2)
            repeats(CHUNKS - 1)
            store_keys(CHUNKS - 2)
            store_keys(CHUNKS - 1)

            def store_queries(part, n):
                act.wait_ge(ring_s, part.ring(("queries", n)))
                src = ps[:, part.bank(("queries", n)), :].bitcast(BF16).rearrange("p (a n) -> p a n", a=2)
                for odd in range(2):
                    rows = slice(SL * odd, SL * odd + SL)
                    last = act.activation(qa[rows, n % 2, odd:HQ:2, :], src[rows, :, :], ACT.Copy)
                last.then_inc(ring_used, 1)

            def store_stack(part, n):
                act.wait_ge(ring_s, part.ring(("stack", n)))
                src = ps[:, part.bank(("stack", n)), :].bitcast(BF16).rearrange("p (a n) -> p a n", a=2)
                act.activation(qb[:, n % 2, :, :], src, ACT.Copy).then_inc(ring_used, 1)

            def store_sums(part, n):
                act.wait_ge(pv_s, part.unit(n, STEPS, STEPS))
                act.activation(ot[:, n % 2, :], ps[:, B_OUT, :], ACT.Copy).then_inc(ot_s, 1)

            def step(part, n, kt):
                if kt == 4 and ("att", n, 0) in part.items:
                    for i, cols in enumerate((slice(0, 256), slice(256, 384), slice(384, 512))):
                        act.wait_ge(ring_s, part.ring(("att", n, i)))
                        act.activation(attT[:, cols], ps[:, part.bank(("att", n, i)), 0:cols.stop - cols.start],
                                       ACT.Copy).then_inc(ring_used, 1)
                if kt == 8 and part.more(n, 2):
                    store_queries(part, n + 2)
                for h in range(HQ):
                    key = ("scores", n, kt, h)
                    act.wait_ge(ring_s, part.ring(key))
                    j = (n * STEPS + kt) * HQ + h
                    if h == 0 and n * STEPS + kt >= PROBS // HQ:
                        act.wait_ge(pv_s, part.unit(n, STEPS, kt - PROBS // HQ + 1))
                    act.activation(probs[:, j % PROBS, :], ps[:, part.bank(key), :], ACT.Exp,
                                   scale=SCALE).then_inc(ring_used, 1)
                if kt == 0 and n >= 1:
                    store_sums(part, n - 1)
                if kt == STEPS - 1 and part.more(n, 1):
                    store_stack(part, n + 1)

            start = before()
            act.wait_ge(pads_s, 2)
            store_queries(start, 0)
            store_queries(start, 1)
            store_stack(start, 0)
            end = attention(act, step)
            store_sums(end, UNITS - 1)
            act.wait_ge(on_s, UNITS + 1)
            act.activation(attT, ps[:, B_RING, :], ACT.Copy).then_inc(ot_s, 1)

            def ffn(s, i):
                q = CHUNKS * s + i
                act.wait_ge(r_s, q + 1)
                if q >= 2:
                    act.wait_ge(xf_s, q - 1)
                act.activation(sg[:, i % 2, :], ps[:, 0 + 3 * (i % 2), :], ACT.Sigmoid).then_inc(sg_s, 1)
                act.wait_ge(kk_s, q + 1)
                if q >= 1:
                    act.wait_ge(ks_s, q)
                act.activation(kr, ps[:, 1 + 3 * (i % 2), :], ACT.Relu).then_inc(kr_s, 1)
                act.wait_ge(kr_s, q + 1)
                if q >= 2:
                    act.wait_ge(v_s, q - 1)
                act.activation(ks[:, i % 2, :], kr, ACT.Square).then_inc(ks_s, 1)

            def ht_tail(stage, i):
                dst = ht1 if stage % 2 == 0 else ht0
                store_ht(CHUNKS * (stage + 1) + i, dst[:, 1 + i * CW:1 + (i + 1) * CW])

            for i in range(CHUNKS + 1):
                if i < CHUNKS:
                    ht_tail(0, i)
                if i >= 1:
                    ffn(0, i - 1)
            for i in range(CHUNKS + 1):
                if i < CHUNKS:
                    ht_tail(1, i)
                if i >= 1:
                    j = i - 1
                    act.wait_ge(q3_s, j + 1)
                    act.activation(qt[:, j * CW:(j + 1) * CW], ps[:, 0, :], ACT.Relu).then_inc(q3a_s, 1)
                    act.wait_ge(kv3_s, j + 1)
                    if j >= 2:
                        act.wait_ge(ctx_s, j - 1)
                    kv = ps[:, 1:3, :].rearrange("p b (t c) -> p (b t) c", t=2)
                    act.activation(kn3[:, j % 2, :, :], kv[:, :, 0:C], ACT.Relu)
                    act.activation(vn3[:, j % 2, :, 0:C], kv[:, :, C:2 * C], ACT.Copy).then_inc(kv3a_s, 1)
            for i in range(CHUNKS):
                act.wait_ge(lt_s, i + 1)
                act.activation(att3[:, i % 2, :], ps[:, 4 + i % 2, :], ACT.Copy).then_inc(lta_s, 1)
                if i >= 1:
                    ht_tail(2, i - 1)
            ht_tail(2, CHUNKS - 1)
            for i in range(CHUNKS):
                ffn(1, i)

        @block.tensor
        def _(pe):
            pe.wait_ge(k_s, 16)
            pe.wait_ge(identb_s, 1)

            def turn_xn(q):
                pe.wait_ge(xn_s, q + 1)
                if q >= 1:
                    pe.wait_ge(ht_s, q)
                for t in range(TPC):
                    last = pe.transpose(ps[:, B_OUT, t * P:(t + 1) * P], xn[:, q % 2, t, :], ident)
                last.then_inc(xt_s, 1)

            def turn_keys(i):
                pe.wait_ge(dups_s, i + 1)
                if i == 0:
                    pe.wait_ge(pads_s, 1)
                for j in range(4):
                    item = 4 * i + j
                    if item >= SCORE_BANKS:
                        pe.wait_ge(kt_used, item - SCORE_BANKS + 1)
                    dst = ps[:, B_RING + item % SCORE_BANKS, :].bitcast(BF16)
                    for a in range(2):
                        for t in range(TPC):
                            pr = 2 * j + a
                            src = kn_rows[:, i * TPC + t, 2 * SL * pr:2 * SL * (pr + 1)]
                            at = a * CW + t * P
                            last = pe.transpose(dst[:, at:at + P], src, identb[:, :])
                    last.then_inc(kt_s, 1)

            for i in range(CHUNKS):
                turn_xn(i)
                pe.wait_ge(ht_s, i + 1)
                if i == 0:
                    pe.wait_ge(w1_s, 16)
                for t in range(TPC):
                    tile = i * TPC + t
                    if tile >= 4:
                        pe.wait_ge(qkv_used, tile - 3)
                    pe.matmul(ps[:, t, 0:3 * C], ht0[:, 1 + tile * P:1 + (tile + 1) * P], wcol("qkv"),
                              start=True, stop=True).then_inc(qkv_s, 1)
                if i >= 2:
                    turn_keys(i - 2)
            turn_keys(CHUNKS - 2)
            turn_keys(CHUNKS - 1)

            def turn_q(n, bank, tiles):
                dst = ps[:, bank, :].bitcast(BF16)
                pe.sem_inc(turns_begun, 1)
                for a in range(2):
                    for t in range(TPC):
                        h = SL * (HQ * (n % QUADS) + 2 * a)
                        last = pe.transpose(dst[:, a * CW + t * P:a * CW + (t + 1) * P],
                                            tiles(t)[:, h:h + 2 * SL], identb[:, :])
                last.then_inc(ring_s, 1)

            def turn_queries(part, n):
                pe.wait_ge(ring_used, part.ring(("queries", n), 1 - SCORE_BANKS))
                turn_q(n, part.bank(("queries", n)), lambda t: q_tile(part.chunk_tile(n, t)))

            def turn_stack(part, n):
                pe.wait_ge(ring_used, part.ring(("stack", n), 1 - SCORE_BANKS))
                pe.wait_ge(max_s, part.unit(n, 1, 1))
                turn_q(n, part.bank(("stack", n)), lambda t: q_tile(part.chunk_tile(n, t)))

            def q_tile(tile):
                return qn_rows[:, bass.ds(tile, 1), :].rearrange("p a s -> p (a s)")

            def max_scores(part, n, s, begin=False):
                t, j = divmod(s, TPC)
                g = n % QUADS
                for pr in range(2):
                    if not (begin and n == 0 and s == 0):
                        pe.wait_ge(pair_used, part.unit(n, 2 * STEPS, 2 * s + pr - 1))
                    for a in range(2):
                        last = pe.matmul(ps[:, B_PAIR + 2 * pr + a, :], qa[:, n % 2, 2 * pr + a, t * P:(t + 1) * P],
                                         kb[:, 2 * g + pr, j * CW:(j + 1) * CW], start=True, stop=True)
                    last.then_inc(pair_s, 1)

            def sums(part, n, kt):
                g = n % QUADS
                if kt == 0 and n >= 1:
                    pe.wait_ge(ot_s, part.unit(n, 1, 0))
                pe.wait_ge(ring_used, part.ring(("scores", n, kt, HQ - 1)))
                for h in range(HQ):
                    j = (n * STEPS + kt) * HQ + h
                    last = pe.matmul(ps[32 * h:32 * h + 32, B_OUT, :], vt[:, kt, HQ * g + h, :],
                                     probs[:, j % PROBS, :], start=(kt == 0), stop=(kt == STEPS - 1))
                last.then_inc(pv_s, 1)

            def turn_sums(part, n, pairs):
                pe.wait_ge(ot_s, part.unit(n, 1, 1))
                pe.wait_ge(pair_used, pairs)
                for t in range(TPC):
                    last = pe.transpose(ps[:, B_PAIR, t * P:(t + 1) * P], ot[:, n % 2, t * P:(t + 1) * P], ident)
                last.then_inc(on_s, 1)

            def step(part, n, kt):
                a = part.a_step(n, kt)
                if a is not None:
                    if kt == 3 and n >= 1:
                        pe.wait_ge(attn_s, part.unit(n, 1, 0))
                    if kt == 7 and n >= 1 and n % QUADS == 0:
                        pe.wait_ge(x1_s, part.unit(n, 1, 0) // QUADS if part.per else n // QUADS)
                    if a[1] == 0:
                        pe.wait_ge(ring_used, part.ring(("queries", a[0])) if ("queries", a[0]) in part.items
                                   else RING0 - 1)
                    max_scores(part, *a)
                if kt == 4 and n >= 1 and n % QUADS == 0:
                    turn_attn(part, n)
                if kt == 8 and part.more(n, 2):
                    turn_queries(part, n + 2)
                for h in range(HQ):
                    key = ("scores", n, kt, h)
                    free = part.ring(key, 1 - SCORE_BANKS)
                    if kt == 0 and h == 0:
                        pe.wait_ge(ring_used, part.ring(key, 0))
                    else:
                        pe.wait_ge(ring_used, free)
                    rows = slice(SL * (h % 2), SL * (h % 2) + SL)
                    pe.matmul(ps[:, part.bank(key), :], kb[rows, 2 * (n % QUADS) + h // 2, kt * P:(kt + 1) * P],
                              qb[rows, n % 2, h // 2, :], start=True, stop=True).then_inc(ring_s, 1)
                if kt >= 1:
                    sums(part, n, kt - 1)
                elif n > part.first:
                    sums(part, n - 1, STEPS - 1)
                elif n >= 1:
                    carried_sums(part, n)
                if kt == 2 and n >= 1:
                    s = n * STEPS + kt + LEAD
                    pairs = part.unit(n, 2 * STEPS, 2 * (kt + LEAD) + 1) if part.a_step(n, kt) else 2 * UNITS * STEPS
                    turn_sums(part, n - 1, pairs)
                if kt == 6 and n >= 1 and n % QUADS == 0:
                    project(part, n)
                if kt == STEPS - 1 and part.more(n, 1):
                    turn_stack(part, n + 1)

            def carried_sums(part, n):
                g = (n - 1) % QUADS
                pe.wait_ge(ring_used, part.ring(("scores", n, 0, 0), -1))
                for h in range(HQ):
                    j = ((n - 1) * STEPS + STEPS - 1) * HQ + h
                    last = pe.matmul(ps[32 * h:32 * h + 32, B_OUT, :], vt[:, STEPS - 1, HQ * g + h, :],
                                     probs[:, j % PROBS, :], start=False, stop=True)
                last.then_inc(pv_s, 1)

            def turn_attn(part, n):
                pe.wait_ge(attn_s, part.unit(n, 1, 0))
                for i, tiles in enumerate(((0, 1), (2,), (3,))):
                    pe.wait_ge(ring_used, part.ring(("att", n, i), 1 - SCORE_BANKS))
                    for j, t in enumerate(tiles):
                        last = pe.transpose(ps[:, part.bank(("att", n, i)), j * P:(j + 1) * P], attn[:, t, :], ident)
                    last.then_inc(ring_s, 1)

            def project(part, n):
                pe.wait_ge(ring_used, part.ring(("att", n, 2)))
                pe.wait_ge(pair_used, part.unit(n, 2 * STEPS, 2 * (6 + LEAD) + 1))
                for t in range(TPC):
                    last = pe.matmul(ps[:, B_PAIR, t * P:(t + 1) * P], attT[:, t * P:(t + 1) * P], wcol("proj"),
                                     start=True, stop=True)
                last.then_inc(proj_s, 1)

            start = before()
            pe.wait_ge(kt_used, 4 * CHUNKS)
            for n in range(2):
                turn_q(n, start.bank(("queries", n)), q_tile)
            pe.wait_ge(qkv_used, NT)
            for s in range(LEAD):
                if s % STEPS == 0:
                    pe.wait_ge(ring_used, s // STEPS + 1)
                max_scores(start, s // STEPS, s % STEPS, begin=True)
            pe.wait_ge(max_s, 1)
            turn_q(0, start.bank(("stack", 0)), q_tile)
            pe.wait_ge(pads_s, 2)
            pe.wait_ge(w2_s, 16)
            end = attention(pe, step)
            sums(end, UNITS - 1, STEPS - 1)
            pe.wait_ge(attn_s, UNITS - 1)
            turn_sums(end, UNITS - 1, 2 * UNITS * STEPS)
            pe.wait_ge(attn_s, UNITS)
            for t in range(TPC):
                last = pe.transpose(ps[:, B_RING, t * P:(t + 1) * P], attn[:, t, :], ident)
            last.then_inc(on_s, 1)
            pe.wait_ge(ot_s, UNITS + 1)
            for t in range(TPC):
                last = pe.matmul(ps[:, B_PAIR, t * P:(t + 1) * P], attT[:, t * P:(t + 1) * P], wcol("proj"),
                                 start=True, stop=True)
            last.then_inc(proj_s, 1)

            def natural(bank, groups, width=P):
                for t in range(TPC):
                    for m, (z, at, wt) in enumerate(groups):
                        last = pe.matmul(ps[:, bank, t * width:(t + 1) * width], z[:, at + t * P:at + (t + 1) * P],
                                         wt, start=(m == 0), stop=(m == len(groups) - 1))
                return last

            def ffn_rk(s, ht, i):
                q = CHUNKS * s + i
                b = 3 * (i % 2)
                pe.wait_ge(ht_s, CHUNKS * (1 + 2 * s) + i + 1)
                if q >= 2:
                    pe.wait_ge(ks_s, q - 1)
                natural(b, ((ht, 1 + i * CW, wmix[:, 0, :]), (ht, i * CW, wmix[:, 1, :]))).then_inc(r_s, 1)
                pe.matmul(ps[:, b + 1, :], wmix[:, 2, :], ht[:, 1 + i * CW:1 + (i + 1) * CW], start=True, stop=False)
                pe.matmul(ps[:, b + 1, :], wmix[:, 3, :], ht[:, i * CW:(i + 1) * CW], start=False,
                          stop=True).then_inc(kk_s, 1)

            def ffn_v(s, i):
                q = CHUNKS * s + i
                pe.wait_ge(ks_s, q + 1)
                if q >= 2:
                    pe.wait_ge(xf_s, q - 1)
                natural(2 + 3 * (i % 2), ((ks[:, i % 2, :], 0, wcol("v")),)).then_inc(v_s, 1)

            pe.wait_ge(mix_s, 1)
            pe.wait_ge(x1_s, CHUNKS)
            for i in range(CHUNKS + 2):
                if i < CHUNKS:
                    turn_xn(CHUNKS + i)
                if 1 <= i <= CHUNKS:
                    ffn_rk(0, ht1, i - 1)
                if i >= 2:
                    ffn_v(0, i - 2)
            pe.wait_ge(xf_s, CHUNKS)
            for i in range(CHUNKS + 2):
                if i < CHUNKS:
                    turn_xn(2 * CHUNKS + i)
                if 1 <= i <= CHUNKS:
                    j = i - 1
                    pe.wait_ge(ht_s, 2 * CHUNKS + j + 1)
                    if j >= 1:
                        pe.wait_ge(kv3a_s, j)
                    pe.matmul(ps[:, 0, :], wcol("lin_qkv", 0, C), ht0[:, 1 + j * CW:1 + (j + 1) * CW],
                              start=True, stop=True).then_inc(q3_s, 1)
                    for t in range(TPC):
                        last = pe.matmul(ps[:, 1 + t // 2, (t % 2) * 2 * C:(t % 2 + 1) * 2 * C],
                                         ht0[:, 1 + j * CW + t * P:1 + j * CW + (t + 1) * P],
                                         wcol("lin_qkv", C, 3 * C), start=True, stop=True)
                    last.then_inc(kv3_s, 1)
                if i >= 2:
                    j = i - 2
                    pe.wait_ge(kv3a_s, j + 1)
                    for t in range(TPC):
                        last = pe.matmul(ps[:, 3, 0:C + 1], kn3[:, j % 2, t, :], vn3[:, j % 2, t, 0:C + 1],
                                         start=(j == 0 and t == 0), stop=(j == CHUNKS - 1 and t == TPC - 1))
                    last.then_inc(ctx_s, 1)
            pe.wait_ge(ctxm_s, 1)

            def lin_out(i):
                if i >= 1:
                    pe.wait_ge(ln_s, i)
                for t in range(TPC):
                    last = pe.matmul(ps[:, t // 2, (t % 2) * 256:(t % 2) * 256 + C + H],
                                     qt[:, i * CW + t * P:i * CW + (t + 1) * P], ctxm, start=True, stop=True)
                last.then_inc(lo_s, 1)

            def lin_turn(i):
                pe.wait_ge(ln_s, i + 1)
                if i >= 2:
                    pe.wait_ge(lta_s, i - 1)
                for t in range(TPC):
                    last = pe.transpose(ps[:, 4 + i % 2, t * P:(t + 1) * P], at3[:, i % 2, t, :], ident)
                last.then_inc(lt_s, 1)

            def lin_proj(i):
                pe.wait_ge(lta_s, i + 1)
                if i >= 1:
                    pe.wait_ge(lx_s, i)
                natural(6, ((att3[:, i % 2, :], 0, wcol("lin_proj")),)).then_inc(lp_s, 1)

            pe.wait_ge(q3a_s, CHUNKS)
            lin_out(0)
            for i in range(CHUNKS):
                lin_turn(i)
                if i + 1 < CHUNKS:
                    lin_out(i + 1)
                lin_proj(i)
                if i >= 1:
                    turn_xn(3 * CHUNKS + i - 1)
            turn_xn(4 * CHUNKS - 1)
            for i in range(CHUNKS + 1):
                if i < CHUNKS:
                    ffn_rk(1, ht1, i)
                if i >= 1:
                    ffn_v(1, i - 1)

        @block.vector
        def _(dve):
            links = [0]

            def link(ins):
                links[0] += 1
                ins.then_inc(chain, 1)
                dve.wait_ge(chain, links[0])

            dve.wait_ge(k_s, 16)
            dve.tensor_copy(identb[:, :], ident).then_inc(identb_s, 1)

            def ln_stats(q, i):
                if q >= 1:
                    dve.wait_ge(stats_s, q)
                if q >= 2:
                    dve.wait_ge(xn_s, q - 1)
                for t in range(TPC):
                    ins = dve.bn_stats(stats[:, t, :], x[:, i * TPC + t, :])
                link(ins)
                for t in range(TPC):
                    ins = dve.bn_aggr(mv[:, q % 2, t, :], stats[:, t, :])
                ins.then_inc(stats_s, 1)

            def ln_apply(q, i):
                dve.wait_ge(rstd_s, q + 1)
                dve.wait_ge(stats_s, q + 1)
                if q >= 2:
                    dve.wait_ge(xt_s, q - 1)
                for t in range(TPC):
                    ins = dve.tensor_scalar(xn[:, q % 2, t, :], x[:, i * TPC + t, :], mv[:, q % 2, t, 0:1],
                                            rstd[:, q % 2, t:t + 1], ALU.subtract, ALU.mult)
                ins.then_inc(xn_s, 1)

            def qkv_store(i):
                if i == 0:
                    dve.wait_ge(w1_s, 16)
                for t in range(TPC):
                    tile = i * TPC + t
                    dve.wait_ge(qkv_s, tile + 1)
                    dve.tensor_tensor(qk[:, t, :], ps[:, t, 0:2 * C], wcol("qkv_b", 0, 2 * C), ALU.add)
                    ins = dve.tensor_tensor(vt[:, tile, :, 0:D], ps[:, t, 2 * C:3 * C].rearrange("p (h d) -> p h d", h=H),
                                            wcol("qkv_b", 2 * C, 3 * C).rearrange("p (h d) -> p h d", h=H), ALU.add)
                    ins.then_inc(qkv_used, 1)
                dve.wait_ge(qkv_used, (i + 1) * TPC)

            def rope(i):
                v = qk.rearrange("p t (g j two) -> p t g j two", g=2 * H, two=2)
                r = rot.rearrange("p t (g j two) -> p t g j two", g=2 * H, two=2)
                e, od = v[:, :, :, :, 0], v[:, :, :, :, 1]
                m = tmp.rearrange("p t (two g j) -> p t g j two", two=2, g=2 * H)
                m0, m1 = m[:, :, :, :, 0], m[:, :, :, :, 1]
                tt = slice(i * TPC, (i + 1) * TPC)
                cs = cos[:, tt, :].unsqueeze(2).broadcast_to([P, TPC, 2 * H, D // 2])
                sn = sin[:, tt, :].unsqueeze(2).broadcast_to([P, TPC, 2 * H, D // 2])
                dve.tensor_tensor(m0, od, sn, ALU.mult)
                dve.tensor_tensor(m1, od, cs, ALU.mult)
                dve.tensor_tensor(r[:, :, :, :, 0], e, cs, ALU.mult)
                link(dve.tensor_tensor(r[:, :, :, :, 1], e, sn, ALU.mult))
                dve.tensor_tensor(r[:, :, :, :, 0], r[:, :, :, :, 0], m0, ALU.subtract)
                link(dve.tensor_tensor(r[:, :, :, :, 1], r[:, :, :, :, 1], m1, ALU.add))

            def split(i):
                t = slice(i * TPC, (i + 1) * TPC)
                r = rot.rearrange("p t (z h d) -> p t z h d", z=2, h=H)
                q, k, qs, ks_ = r[:, :, 0], r[:, :, 1], qn[:, t], kn[:, t]
                dve.tensor_copy(qs[:, :, :, 0:D], q)
                link(dve.tensor_copy(ks_[:, :, :, 0:D], k))
                dve.tensor_tensor(q, q, qs[:, :, :, 0:D], ALU.subtract)
                link(dve.tensor_tensor(k, k, ks_[:, :, :, 0:D], ALU.subtract))
                dve.tensor_copy(qs[:, :, :, 16:16 + D], q)
                link(dve.tensor_copy(ks_[:, :, :, 8:8 + D], k))
                dve.tensor_tensor(qs[:, :, :, S_C + 8:S_C + 8 + D], q, qs[:, :, :, 16:16 + D], ALU.subtract)
                dve.tensor_tensor(ks_[:, :, :, S_C:S_C + D], k, ks_[:, :, :, 8:8 + D], ALU.subtract).then_inc(split_s, 1)

            def take_x(i):
                dve.wait_ge(x_in_s[i], 16)
                ln_stats(i, i)

            take_x(0)
            for i in range(CHUNKS):
                ln_apply(i, i)
                if i + 1 < CHUNKS:
                    take_x(i + 1)
                qkv_store(i)
                rope(i)
                split(i)
            dve.wait_ge(w2_s, 16)
            pb = wcol("proj_b").unsqueeze(1).broadcast_to([P, NT, C])
            link(dve.tensor_tensor(x[:, :, :], x[:, :, :], pb, ALU.add))

            def take_max(part, n, s):
                t, j = divmod(s, TPC)
                for pr in range(2):
                    dve.wait_ge(pair_s, part.unit(n, 2 * STEPS, 2 * s + pr + 1))
                    dve.tensor_reduce(mpart[:, n % 2, t, 2 * pr:2 * pr + 2, j], ps[:, B_PAIR + 2 * pr:B_PAIR + 2 * pr + 2, :],
                                      AX.X, ALU.max).then_inc(pair_used, 1)

            LINKS_PER_UNIT = 3

            def put_max(part, n):
                g = n % QUADS
                before_ = part.unit(n, LINKS_PER_UNIT, links[0] - (1 if n else 0))
                dve.wait_ge(pair_used, part.unit(n, 2 * STEPS, 2 * STEPS))
                dve.tensor_reduce(negm[:, :, :], mpart[:, n % 2], AX.X, ALU.max, negate=True).then_inc(chain, 1)
                dve.wait_ge(chain, before_ + 1)
                tiles = bass.ds(part.chunk_tile(n, 0), TPC)
                slot = qn[:, tiles, HQ * g:HQ * g + HQ, S_MAX]
                dve.tensor_copy(slot, negm[:, :, :]).then_inc(chain, 1)
                dve.wait_ge(chain, before_ + 2)
                dve.tensor_tensor(qn[:, tiles, HQ * g:HQ * g + HQ, S_MAX + 1], negm[:, :, :], slot,
                                  ALU.subtract).then_inc(max_s, 1)

            def scale_sums(part, n):
                g = n % QUADS
                dve.wait_ge(on_s, part.unit(n, 1, 1))
                v = ps[:, B_PAIR, :].rearrange("p (t h s) -> p t h s", t=TPC, h=HQ)
                dve.reciprocal(rsum[:, :, :], v[:, :, :, D]).then_inc(chain, 1)
                ahead = min(n + 2, UNITS) if not part.per else None
                if ahead is not None:
                    dve.wait_ge(chain, links[0] + 2 * ahead + n + 1)
                else:
                    dve.wait_ge(chain, part.unit(n, LINKS_PER_UNIT, links[0] + 5))
                out_ = attn[:, :, 32 * g:32 * g + 32].rearrange(
                    "p t (h d) -> p t h d", h=HQ)
                dve.tensor_tensor(out_, v[:, :, :, 0:D], rsum[:, :, :].unsqueeze(3).broadcast_to([P, TPC, HQ, D]),
                                  ALU.mult).then_inc(attn_s, 1)

            def add_proj(part, n):
                dve.wait_ge(proj_s, part.unit(n, 1, 0) // QUADS if part.per else n // QUADS)
                tiles = x[:, bass.ds(part.chunk_tile(n, -TPC), TPC), :]
                dve.tensor_tensor(tiles, tiles, ps[:, B_PAIR, :].rearrange("p (t c) -> p t c", t=TPC),
                                  ALU.add).then_inc(x1_s, 1)

            def step(part, n, kt):
                a = part.a_step(n, kt)
                if a is not None:
                    take_max(part, *a)
                    if a[1] == STEPS - 1:
                        put_max(part, a[0])
                if kt == 2 and n >= 1:
                    scale_sums(part, n - 1)
                if kt == 6 and n >= 1 and n % QUADS == 0:
                    add_proj(part, n)

            start = before()
            for s in range(LEAD):
                take_max(start, s // STEPS, s % STEPS)
                if s % STEPS == STEPS - 1:
                    put_max(start, s // STEPS)
            end = attention(dve, step)
            scale_sums(end, UNITS - 1)
            links[0] += 3 * UNITS
            dve.wait_ge(proj_s, CHUNKS)
            tiles = x[:, NT - TPC:NT, :]
            dve.tensor_tensor(tiles, tiles, ps[:, B_PAIR, :].rearrange("p (t c) -> p t c", t=TPC),
                              ALU.add).then_inc(x1_s, 1)
            dve.wait_ge(x1_s, CHUNKS)

            link(dve.tensor_scalar(onem, wcol("mu"), -1.0, 1.0, ALU.mult, ALU.add))
            for m, name in enumerate(("r", "k")):
                dve.tensor_scalar(wmix[:, 2 * m, :], wcol(name), wcol("mu", m, m + 1), None, ALU.mult)
                dve.tensor_scalar(wmix[:, 2 * m + 1, :], wcol(name), onem[:, m:m + 1], None, ALU.mult)
            dve.memset(ht1[:, 0:1], 0.0)
            dve.memset(vn3[:, :, :, C:C + 1], 1.0)
            dve.memset(ht0[:, 0:1], 0.0).then_inc(mix_s, 1)

            def ffn_add(s, i):
                q = CHUNKS * s + i
                t = slice(i * TPC, (i + 1) * TPC)
                dve.wait_ge(sg_s, q + 1)
                dve.wait_ge(v_s, q + 1)
                link(dve.tensor_tensor(vs, ps[:, 2 + 3 * (i % 2), :], sg[:, i % 2, :], ALU.mult))
                dve.tensor_tensor(x[:, t, :], x[:, t, :], vs.rearrange("p (t c) -> p t c", t=TPC),
                                  ALU.add).then_inc(xf_s, 1)
                dve.wait_ge(xf_s, q + 1)

            ln_stats(CHUNKS, 0)
            for i in range(CHUNKS):
                if i + 1 < CHUNKS:
                    ln_stats(CHUNKS + i + 1, i + 1)
                ln_apply(CHUNKS + i, i)
            for i in range(CHUNKS + 1):
                if i < CHUNKS:
                    ffn_add(0, i)
                    ln_stats(2 * CHUNKS + i, i)
                if i >= 1:
                    ln_apply(2 * CHUNKS + i - 1, i - 1)
            pb3 = wcol("lin_proj_b").unsqueeze(1).broadcast_to([P, NT, C])
            dve.wait_ge(xn_s, 3 * CHUNKS)
            link(dve.tensor_tensor(x[:, :, :], x[:, :, :], pb3, ALU.add))
            dve.wait_ge(ctx_s, CHUNKS)
            dve.tensor_tensor(ctxm[:, 0:C], block_mask, ps[:, 3, 0:C], ALU.mult)
            link(dve.tensor_copy(ksum, ps[:, 3, C:C + 1]))
            heads = block_mask.rearrange("p (h d) -> p h d", h=H)[:, :, 0]
            dve.tensor_scalar(ctxm[:, C:C + H], heads, ksum, None, ALU.mult).then_inc(ctxm_s, 1)

            def lin_scale(i):
                dve.wait_ge(lo_s, i + 1)
                if i >= 2:
                    dve.wait_ge(lt_s, i - 1)
                v = ps[:, 0:2, :].rearrange("p b (t c) -> p (b t) c", t=2)
                link(dve.tensor_scalar(zz[:, 0], v[:, :, C:C + H], Z_EPS, None, ALU.add))
                link(dve.reciprocal(zz[:, 1], zz[:, 0]))
                dve.tensor_tensor(at3[:, i % 2].rearrange("p t (h d) -> p t h d", h=H),
                                  v[:, :, 0:C].rearrange("p t (h d) -> p t h d", h=H),
                                  zz[:, 1].unsqueeze(3).broadcast_to([P, TPC, H, D]), ALU.mult).then_inc(ln_s, 1)

            def lin_add(i):
                t = slice(i * TPC, (i + 1) * TPC)
                dve.wait_ge(lp_s, i + 1)
                dve.tensor_tensor(x[:, t, :], x[:, t, :], ps[:, 6, :].rearrange("p (t c) -> p t c", t=TPC),
                                  ALU.add).then_inc(lx_s, 1)
                dve.wait_ge(lx_s, i + 1)
                ln_stats(3 * CHUNKS + i, i)

            lin_scale(0)
            for i in range(CHUNKS):
                if i + 1 < CHUNKS:
                    lin_scale(i + 1)
                lin_add(i)
                ln_apply(3 * CHUNKS + i, i)
            for i in range(CHUNKS):
                ffn_add(1, i)


def rope_tables():
    import numpy as np
    inv = (np.float32(1.0) / np.float32(10000.0) ** (np.arange(0, D, 2, dtype=np.float32) / np.float32(D))).astype(np.float32)
    freqs = (np.arange(N, dtype=np.float32)[:, None] * inv[None, :]).astype(np.float32)

    def lay(z):
        return z.astype(np.float32).reshape(NT, P, D // 2).transpose(1, 0, 2).reshape(P, NT * D // 2)
    return lay(np.cos(freqs.astype(np.float64))), lay(np.sin(freqs.astype(np.float64)))


def kernel(**inputs):
    import numpy as np
    import concourse.bacc as bacc
    from concourse.bass_utils import run_bass_kernel_spmd

    g = {k: np.asarray(v) for k, v in inputs.items()}

    def rows(v):
        return np.broadcast_to(v[None, :], (P, v.shape[0]))

    parts = {
        "qkv": g["L0_attn_a_qkv_w"].T, "qkv_b": rows(g["L0_attn_a_qkv_b"]), "proj": g["L0_attn_a_proj_w"].T,
        "proj_b": rows(g["L0_attn_a_proj_b"]), "lin_qkv": g["L0_attn_b_w_qkv"].T, "lin_proj": g["L0_attn_b_w_proj"].T,
        "lin_proj_b": rows(g["L0_attn_b_b_proj"]), "r": g["L0_ffn_W_r"].T, "k": g["L0_ffn_W_k"].T,
        "v": g["L0_ffn_W_v"].T, "mu": np.stack([g["L0_ffn_mu_r"], g["L0_ffn_mu_k"]], axis=1),
    }
    weights = np.ascontiguousarray(np.concatenate([parts[n] for n in W_COLS], axis=1))
    cos, sin = rope_tables()
    head = np.arange(P) // D
    consts = np.ascontiguousarray(np.concatenate(
        [cos, sin, np.eye(P, dtype=np.float32), (head[:, None] == head[None, :]).astype(np.float32)], axis=1))
    xs = np.ascontiguousarray(g["L0_attn_a_x"].reshape(N, C))

    nc = bacc.Bacc("TRN2", target_bir_lowering=False, num_devices=1)
    arrays = {"x_dram": xs, "w_dram": weights, "k_dram": consts}
    args = [nc.dram_tensor(n, a.shape, mybir.dt.from_np(a.dtype), kind="ExternalInput").ap() for n, a in arrays.items()]
    out = nc.dram_tensor("out_dram", (N, C), F32, kind="ExternalOutput").ap()
    build(nc, *args, out)
    r = run_bass_kernel_spmd(nc, [arrays], core_ids=[0])
    return r.results[0]["out_dram"].reshape(1, N, C)
```

```python
from contextlib import ExitStack

import concourse.bass as bass
from concourse import mybir

ALU = mybir.AluOpType
ACT = mybir.ActivationFunctionType
AX = mybir.AxisListType
F32 = mybir.dt.float32
BF16 = mybir.dt.bfloat16

P = 128
N = 2048
C = 128
H = 16
D = C // H
NT = N // P
CHUNKS = 4
TPC = NT // CHUNKS
CW = N // CHUNKS
QUADS = 4
HQ = H // QUADS
UNITS = CHUNKS * QUADS
STEPS = NT
LN_EPS = 1e-5
Z_EPS = 2.0 ** -23
SCALE = float(D) ** -0.5

SL = 64
S_MAX = 32
S_C = 40

SCORE_BANKS = 3
PROBS = 8
LEAD = STEPS + 3

SUMS_STEP = 2
ATT_STEP = 4
PROJ_STEP = 6
QUERY_STEPS = (8, 10)
STACK_STEP = 14

B_PAIR = 0
B_RING = 4
B_OUT = 7

W_COLS = {}
for _name, _n in (("qkv", 3 * C), ("qkv_b", 3 * C), ("proj", C), ("proj_b", C), ("lin_qkv", 3 * C), ("lin_proj", C),
                  ("lin_proj_b", C), ("r", C), ("k", C), ("v", C), ("mu", 2)):
    W_COLS[_name] = (sum(n for _, n in W_COLS.values()), _n)
W_TOTAL = sum(n for _, n in W_COLS.values())
W_FIRST = 6 * C
K_COS, K_SIN, K_IDENT, K_BLOCK, K_TOTAL = 0, 64, 128, 256, 384


def ring_places(first, last):
    places, at = {}, 0
    for n in range(first, last + 1):
        for kt in range(STEPS):
            before, after = [], []
            if kt == ATT_STEP and n % QUADS == 0 and n > 0:
                before = [("att", n, t) for t in range(TPC)]
            if kt in QUERY_STEPS and n + 2 < UNITS:
                before = [("queries", n + 2, QUERY_STEPS.index(kt))]
            if kt == STACK_STEP and n + 1 < UNITS:
                before, after = [("stack", n + 1, 0)], [("stack", n + 1, 1)]
            for key in before + [("scores", n, kt, h) for h in range(HQ)] + after:
                places[key] = at
                at += 1
    return places, at


def build(nc, x_in, w_in, k_in, out):
    ctx = ExitStack()
    with ctx:
        def sb(name, shape, dt):
            return ctx.enter_context(nc.sbuf_tensor(name, shape, dt))

        def sem(name):
            return ctx.enter_context(nc.semaphore(name))

        ps = ctx.enter_context(nc.psum_tensor("ps", [P, 8, 512], F32))
        w = sb("w", [P, W_TOTAL], F32)
        kc = sb("kc", [P, K_TOTAL], F32)
        identb = sb("identb", [P, P], BF16)
        x = sb("x", [P, NT, C], F32)
        stats = sb("stats", [P, TPC, 6], F32)
        mv = sb("mv", [P, 2, TPC, 2], F32)
        ve = sb("ve", [P, TPC], F32)
        neghalf = sb("neghalf", [P, TPC], F32)
        rstd = sb("rstd", [P, 2, TPC], F32)
        xn = sb("xn", [P, 2, TPC, C], F32)
        ht0 = sb("ht0", [P, N + 1], F32)
        kb = sb("kb", [P, H // 2, N], BF16)
        vt = sb("vt", [P, NT, H, 32], F32)
        qa = sb("qa", [P, 2, HQ, CW], BF16)
        qb = sb("qb", [P, 2, 2, CW], BF16)
        mpart = sb("mpart", [P, 2, TPC, HQ, TPC], F32)
        negm = sb("negm", [P, TPC, HQ], F32)
        rsum = sb("rsum", [P, TPC, HQ], F32)
        qn_raw = sb("qn_raw", [P, NT * H * SL // 2], F32)
        kn_raw = sb("kn_raw", [P, NT * H * SL // 2], F32)
        first = sb("first", [P, 3, TPC, 2 * C], F32)

        qn = qn_raw[:, :].bitcast(BF16).rearrange("p (t h s) -> p t h s", t=NT, h=H)
        kn = kn_raw[:, :].bitcast(BF16).rearrange("p (t h s) -> p t h s", t=NT, h=H)
        kn_rows = kn_raw[:, :].bitcast(BF16).rearrange("p (t s) -> p t s", t=NT)
        qn_rows = qn_raw[:, :].bitcast(BF16).rearrange("p (t s) -> p t s", t=NT)
        qk, rot, tmp = first[:, 0], first[:, 1], first[:, 2]
        probs = kn_raw[:, 0:PROBS * 512].rearrange("p (b n) -> p b n", b=PROBS)
        at = PROBS * 512
        ot = kn_raw[:, at:at + 2 * 512].rearrange("p (b n) -> p b n", b=2)
        at += 2 * 512
        attn = kn_raw[:, at:at + CW].rearrange("p (t c) -> p t c", t=TPC)
        at += CW
        attT = kn_raw[:, at:at + 512]

        def wcol(name, a=0, b=None):
            at, n = W_COLS[name]
            return w[:, at + a:at + (n if b is None else b)]

        ident = kc[:, K_IDENT:K_IDENT + P]
        cos = kc[:, K_COS:K_COS + 64].rearrange("p (t i) -> p t i", t=NT)
        sin = kc[:, K_SIN:K_SIN + 64].rearrange("p (t i) -> p t i", t=NT)
        block_mask = kc[:, K_BLOCK:K_BLOCK + P]

        ht1 = qn_raw[:, 0:N + 1]
        qt = qn_raw[:, N + 4:2 * N + 4]
        o = 2 * N + 4
        sg = qn_raw[:, o:o + 1024].rearrange("p (b n) -> p b n", b=2)
        kr = qn_raw[:, o + 1024:o + 1536]
        ks = qn_raw[:, o + 1536:o + 2560].rearrange("p (b n) -> p b n", b=2)
        vs = qn_raw[:, o + 2560:o + 3072]
        kn3 = kn_raw[:, 0:1024].rearrange("p (b t c) -> p b t c", b=2, t=TPC)
        vn3 = kn_raw[:, 1024:1024 + 2 * TPC * 132].rearrange("p (b t c) -> p b t c", b=2, t=TPC)
        at3 = kn_raw[:, 2112:3136].rearrange("p (b t c) -> p b t c", b=2, t=TPC)
        att3 = kn_raw[:, 3136:4160].rearrange("p (b n) -> p b n", b=2)
        zz = kn_raw[:, 4160:4160 + 2 * TPC * H].rearrange("p (a t h) -> p a t h", a=2, t=TPC)
        ctxm = kn_raw[:, 4300:4300 + C + H]
        ksum = kn_raw[:, 4450:4451]
        wmix = first[:, 0:1].rearrange("p a t c -> p (a t c)")[:, 0:4 * C].rearrange("p (m c) -> p m c", m=4)
        onem = first[:, 0, 2, 0:2]

        x_in_s = [sem(f"x_loaded{i}") for i in range(CHUNKS)]
        w1_s, w2_s, k_s = sem("first_weights_loaded"), sem("other_weights_loaded"), sem("constants_loaded")
        identb_s = sem("identb_ready")
        pads_s = sem("pads_ready")
        half_s = sem("neghalf_ready")
        stats_s = sem("ln_stats_ready")
        ve_s = sem("pool_chain")
        rstd_s = sem("rstd_ready")
        xn_s = sem("xn_ready")
        xt_s = sem("xn_turned")
        ht_s = sem("ht_ready")
        qkv_s = sem("qkv_ready")
        qkv_used = sem("qkv_used")
        split_s = sem("split_ready")
        dups_s = sem("dups_ready")
        turns_begun = sem("turns_begun")
        kt_s = sem("keys_turned")
        kt_used = sem("keys_stored")
        chain = sem("dve_chain")
        pair_s = sem("pair_ready")
        pair_used = sem("pair_used")
        max_s = sem("max_ready")
        ring_s = sem("ring_ready")
        ring_used = sem("ring_used")
        pv_s = sem("sums_step_done")
        ot_s = sem("sums_stored")
        on_s = sem("sums_turned")
        attn_s = sem("attn_ready")
        proj_s = sem("proj_ready")
        x1_s = sem("x1_ready")
        mix_s = sem("mixed_weights_ready")
        r_s, kk_s, v_s = sem("r_ready"), sem("k_ready"), sem("v_ready")
        sg_s, kr_s, ks_s = sem("sigmoid_ready"), sem("relu_ready"), sem("square_ready")
        xf_s = sem("ffn_added")
        q3_s, kv3_s = sem("lin_q_ready"), sem("lin_kv_ready")
        q3a_s, kv3a_s = sem("lin_q_stored"), sem("lin_kv_stored")
        ctx_s = sem("context_ready")
        ctxm_s = sem("context_masked")
        lo_s = sem("lin_out_ready")
        ln_s = sem("lin_out_scaled")
        lt_s = sem("lin_out_turned")
        lta_s = sem("lin_out_stored")
        lp_s = sem("lin_proj_ready")
        lx_s = sem("lin_added")
        out_s = sem("out_written")

        block = ctx.enter_context(nc.Block())

        head_items, head_n = ring_places(0, 0)
        body_items, body_n = ring_places(1, QUADS)
        tail_items, _ = ring_places(3 * QUADS + 1, UNITS - 1)
        RING0 = 6
        assert body_n % SCORE_BANKS == 0

        class Part:

            def __init__(self, first, last, items, start, c=0, per_c=0):
                self.first, self.last, self.items, self.start, self.c, self.per = first, last, items, start, c, per_c

            def unit(self, n, times=1, plus=0):
                if self.per:
                    return self.c * (QUADS * times) + (n * times + plus)
                return n * times + plus

            def ring(self, key, plus=1):
                v = self.start + self.items[key] + plus
                return self.c * self.per + v if self.per else v

            def bank(self, key):
                return B_RING + (self.start + self.items[key]) % SCORE_BANKS

            def a_step(self, n, kt):
                s = n * STEPS + kt + LEAD
                if not self.per and s >= UNITS * STEPS:
                    return None
                return s // STEPS, s % STEPS

            def more(self, n, k):
                return bool(self.per) or n + k < UNITS

            def chunk_tile(self, n, t):
                if self.per:
                    return self.c * TPC + (TPC * (n // QUADS) + t)
                return TPC * (n // QUADS) + t

        def attention(eng, step):
            for n in range(0, 1):
                for kt in range(STEPS):
                    step(Part(0, 0, head_items, RING0), n, kt)
            with eng.Fori(0, CHUNKS - 1) as c:
                part = Part(1, QUADS, body_items, RING0 + head_n, c, body_n)
                for n in range(1, QUADS + 1):
                    for kt in range(STEPS):
                        step(part, n, kt)
            start = RING0 + head_n + (CHUNKS - 1) * body_n
            part = Part(3 * QUADS + 1, UNITS - 1, tail_items, start)
            for n in range(3 * QUADS + 1, UNITS):
                for kt in range(STEPS):
                    step(part, n, kt)
            return part

        def before():
            keys = [("queries", n, a) for n in range(2) for a in range(2)] + [("stack", 0, a) for a in range(2)]
            return Part(0, 0, {key: i for i, key in enumerate(keys)}, 0)

        @block.sync
        def _(sp):
            xv = x_in.rearrange("(t p) c -> p t c", p=P)
            ov = out.rearrange("(t p) c -> p t c", p=P)
            sp.dma_start(x[:, 0:TPC, :], xv[:, 0:TPC, :]).then_inc(x_in_s[0], 16)
            sp.dma_start(kc[:, :], k_in).then_inc(k_s, 16)
            sp.dma_start(w[:, 0:W_FIRST], w_in[:, 0:W_FIRST]).then_inc(w1_s, 16)
            for i in range(1, CHUNKS):
                sp.dma_start(x[:, i * TPC:(i + 1) * TPC, :], xv[:, i * TPC:(i + 1) * TPC, :]).then_inc(x_in_s[i], 16)
            sp.dma_start(w[:, W_FIRST:], w_in[:, W_FIRST:]).then_inc(w2_s, 16)
            for i in range(CHUNKS):
                sp.wait_ge(xf_s, CHUNKS + i + 1)
                sp.dma_start(ov[:, i * TPC:(i + 1) * TPC, :], x[:, i * TPC:(i + 1) * TPC, :]).then_inc(out_s, 16)
            sp.wait_ge(out_s, 16 * CHUNKS)

        @block.gpsimd
        def _(pool):
            pool.memset(neghalf[:, :], -0.5).then_inc(half_s, 1)
            for raw in (qn_raw, kn_raw):
                words = raw[:, :].rearrange("p (g s) -> p g s", s=SL // 2)
                pool.memset(words[:, :, S_MAX // 2:S_C // 2], 0.0)
                last = pool.memset(words[:, :, (S_C + 16) // 2:], 0.0)
            last.then_inc(ve_s, 1)
            pool.wait_ge(ve_s, 1)
            pool.memset(kn_raw[:, :].bitcast(BF16).rearrange("p (g s) -> p g s", s=SL)[:, :, S_MAX:S_MAX + 2],
                        1.0).then_inc(pads_s, 1)

            def root(q, links):
                pool.wait_ge(stats_s, q + 1)
                if q >= 1:
                    pool.wait_ge(rstd_s, q)
                pool.tensor_scalar(ve[:, :], mv[:, q % 2, :, 1], LN_EPS, None, ALU.add).then_inc(ve_s, 1)
                pool.wait_ge(ve_s, links)
                pool.tensor_tensor(rstd[:, q % 2, :], ve[:, :], neghalf[:, :], ALU.pow).then_inc(rstd_s, 1)

            pool.wait_ge(half_s, 1)
            root(0, 2)
            pool.memset(vt[:, 0:TPC, :, D:], 0.0)
            pool.memset(qa[:, 0, :, :].bitcast(F32), 0.0)
            root(1, 3)
            pool.memset(vt[:, TPC:2 * TPC, :, D:], 0.0)
            pool.memset(qa[:, 1, :, :].bitcast(F32), 0.0)
            root(2, 4)
            pool.memset(vt[:, 2 * TPC:3 * TPC, :, D:], 0.0)
            root(3, 5)
            pool.memset(vt[:, 3 * TPC:, :, D:], 0.0).then_inc(ve_s, 1)
            pool.wait_ge(ve_s, 6)
            pool.memset(vt[:, :, :, D:D + 1], 1.0).then_inc(pads_s, 1)
            for q in range(CHUNKS, 4 * CHUNKS):
                root(q, q + 3)

        @block.scalar
        def _(act):
            def store_ht(q, dst):
                act.wait_ge(xt_s, q + 1)
                act.activation(dst, ps[:, B_OUT, :], ACT.Copy).then_inc(ht_s, 1)

            def repeats(i):
                act.wait_ge(split_s, i + 1)
                t = slice(i * TPC, (i + 1) * TPC)
                q, k = qn[:, t, :, :], kn[:, t, :, :]
                for z, to, of in ((q, 8, 0), (q, 24, 16), (q, S_C, 0), (k, 16, 0), (k, 24, 8), (k, S_C + 8, 0)):
                    last = act.activation(z[:, :, :, to:to + D], z[:, :, :, of:of + D], ACT.Copy)
                last.then_inc(dups_s, 1)

            def store_keys(i):
                for j in range(4):
                    item = 4 * i + j
                    act.wait_ge(kt_s, item + 1)
                    src = ps[:, B_RING + item % SCORE_BANKS, :].bitcast(BF16).rearrange("p (a n) -> p a n", a=2)
                    cols = slice(i * CW, (i + 1) * CW)
                    act.activation(kb[:, 2 * j:2 * j + 2, cols], src, ACT.Copy).then_inc(kt_used, 1)

            for i in range(CHUNKS):
                store_ht(i, ht0[:, 1 + i * CW:1 + (i + 1) * CW])
                if i >= 1:
                    repeats(i - 1)
                if i >= 2:
                    store_keys(i - 2)
            repeats(CHUNKS - 1)
            store_keys(CHUNKS - 2)
            store_keys(CHUNKS - 1)

            def store_queries(part, n, a):
                act.wait_ge(ring_s, part.ring(("queries", n, a)))
                src = ps[:, part.bank(("queries", n, a)), 0:CW // 2].bitcast(BF16)
                for odd in range(2):
                    rows = slice(SL * odd, SL * odd + SL)
                    last = act.activation(qa[rows, n % 2, 2 * a + odd, :], src[rows, :], ACT.Copy)
                last.then_inc(ring_used, 1)

            def store_stack(part, n, a):
                act.wait_ge(ring_s, part.ring(("stack", n, a)))
                src = ps[:, part.bank(("stack", n, a)), 0:CW // 2].bitcast(BF16)
                act.activation(qb[:, n % 2, a, :], src, ACT.Copy).then_inc(ring_used, 1)

            def store_sums(part, n):
                act.wait_ge(pv_s, part.unit(n, STEPS, STEPS))
                act.activation(ot[:, n % 2, :], ps[:, B_OUT, :], ACT.Copy).then_inc(ot_s, 1)

            def step(part, n, kt):
                if ("att", n, 0) in part.items and kt == ATT_STEP:
                    for t in range(TPC):
                        act.wait_ge(ring_s, part.ring(("att", n, t)))
                        act.activation(attT[:, t * P:(t + 1) * P], ps[:, part.bank(("att", n, t)), 0:P],
                                       ACT.Copy).then_inc(ring_used, 1)
                if kt in QUERY_STEPS and part.more(n, 2):
                    store_queries(part, n + 2, QUERY_STEPS.index(kt))
                if kt == STACK_STEP and part.more(n, 1):
                    store_stack(part, n + 1, 0)
                for h in range(HQ):
                    key = ("scores", n, kt, h)
                    act.wait_ge(ring_s, part.ring(key))
                    j = (n * STEPS + kt) * HQ + h
                    if h == 0 and n * STEPS + kt >= PROBS // HQ:
                        act.wait_ge(pv_s, part.unit(n, STEPS, kt - PROBS // HQ + 1))
                    act.activation(probs[:, j % PROBS, :], ps[:, part.bank(key), :], ACT.Exp,
                                   scale=SCALE).then_inc(ring_used, 1)
                if kt == 0 and n >= 1:
                    store_sums(part, n - 1)
                if kt == STACK_STEP and part.more(n, 1):
                    store_stack(part, n + 1, 1)

            start = before()
            act.wait_ge(pads_s, 2)
            for n in range(2):
                for a in range(2):
                    store_queries(start, n, a)
            for a in range(2):
                store_stack(start, 0, a)
            end = attention(act, step)
            store_sums(end, UNITS - 1)
            act.wait_ge(on_s, UNITS + 1)
            act.activation(attT, ps[:, B_RING, :], ACT.Copy).then_inc(ot_s, 1)

            def ffn(s, i):
                q = CHUNKS * s + i
                act.wait_ge(r_s, q + 1)
                if q >= 2:
                    act.wait_ge(xf_s, q - 1)
                act.activation(sg[:, i % 2, :], ps[:, 0 + 3 * (i % 2), :], ACT.Sigmoid).then_inc(sg_s, 1)
                act.wait_ge(kk_s, q + 1)
                if q >= 1:
                    act.wait_ge(ks_s, q)
                act.activation(kr, ps[:, 1 + 3 * (i % 2), :], ACT.Relu).then_inc(kr_s, 1)
                act.wait_ge(kr_s, q + 1)
                if q >= 2:
                    act.wait_ge(v_s, q - 1)
                act.activation(ks[:, i % 2, :], kr, ACT.Square).then_inc(ks_s, 1)

            def ht_tail(stage, i):
                dst = ht1 if stage % 2 == 0 else ht0
                store_ht(CHUNKS * (stage + 1) + i, dst[:, 1 + i * CW:1 + (i + 1) * CW])

            for i in range(CHUNKS + 1):
                if i < CHUNKS:
                    ht_tail(0, i)
                if i >= 1:
                    ffn(0, i - 1)
            for i in range(CHUNKS + 1):
                if i < CHUNKS:
                    ht_tail(1, i)
                if i >= 1:
                    j = i - 1
                    act.wait_ge(q3_s, j + 1)
                    act.activation(qt[:, j * CW:(j + 1) * CW], ps[:, 0, :], ACT.Relu).then_inc(q3a_s, 1)
                    act.wait_ge(kv3_s, j + 1)
                    if j >= 2:
                        act.wait_ge(ctx_s, j - 1)
                    kv = ps[:, 1:3, :].rearrange("p b (t c) -> p (b t) c", t=2)
                    act.activation(kn3[:, j % 2, :, :], kv[:, :, 0:C], ACT.Relu)
                    act.activation(vn3[:, j % 2, :, 0:C], kv[:, :, C:2 * C], ACT.Copy).then_inc(kv3a_s, 1)
            for i in range(CHUNKS):
                act.wait_ge(lt_s, i + 1)
                act.activation(att3[:, i % 2, :], ps[:, 4 + i % 2, :], ACT.Copy).then_inc(lta_s, 1)
                if i >= 1:
                    ht_tail(2, i - 1)
            ht_tail(2, CHUNKS - 1)
            for i in range(CHUNKS):
                ffn(1, i)

        @block.tensor
        def _(pe):
            pe.wait_ge(k_s, 16)
            pe.wait_ge(identb_s, 1)

            def turn_xn(q):
                pe.wait_ge(xn_s, q + 1)
                if q >= 1:
                    pe.wait_ge(ht_s, q)
                for t in range(TPC):
                    last = pe.transpose(ps[:, B_OUT, t * P:(t + 1) * P], xn[:, q % 2, t, :], ident)
                last.then_inc(xt_s, 1)

            def turn_keys(i):
                pe.wait_ge(dups_s, i + 1)
                if i == 0:
                    pe.wait_ge(pads_s, 1)
                for j in range(4):
                    item = 4 * i + j
                    if item >= SCORE_BANKS:
                        pe.wait_ge(kt_used, item - SCORE_BANKS + 1)
                    dst = ps[:, B_RING + item % SCORE_BANKS, :].bitcast(BF16)
                    for a in range(2):
                        for t in range(TPC):
                            pr = 2 * j + a
                            src = kn_rows[:, i * TPC + t, 2 * SL * pr:2 * SL * (pr + 1)]
                            at = a * CW + t * P
                            last = pe.transpose(dst[:, at:at + P], src, identb[:, :])
                    last.then_inc(kt_s, 1)

            for i in range(CHUNKS):
                turn_xn(i)
                pe.wait_ge(ht_s, i + 1)
                if i == 0:
                    pe.wait_ge(w1_s, 16)
                for t in range(TPC):
                    tile = i * TPC + t
                    if tile >= 4:
                        pe.wait_ge(qkv_used, tile - 3)
                    pe.matmul(ps[:, t, 0:3 * C], ht0[:, 1 + tile * P:1 + (tile + 1) * P], wcol("qkv"),
                              start=True, stop=True).then_inc(qkv_s, 1)
                if i >= 2:
                    turn_keys(i - 2)
            turn_keys(CHUNKS - 2)
            turn_keys(CHUNKS - 1)

            def turn_q(part, key):
                _, n, a = key
                free = part.ring(key, 1 - SCORE_BANKS)
                if not isinstance(free, int) or free > 0:
                    pe.wait_ge(ring_used, free)
                pe.sem_inc(turns_begun, 1)
                dst = ps[:, part.bank(key), :].bitcast(BF16)
                h = SL * (HQ * (n % QUADS) + 2 * a)
                for t in range(TPC):
                    rows = qn_rows[:, bass.ds(part.chunk_tile(n, t), 1), :].rearrange("p a s -> p (a s)")
                    last = pe.transpose(dst[:, t * P:(t + 1) * P], rows[:, h:h + 2 * SL], identb[:, :])
                last.then_inc(ring_s, 1)

            def max_scores(part, n, s, pr):
                t, j = divmod(s, TPC)
                if not (isinstance(part.unit(n), int) and n == 0 and s == 0):
                    pe.wait_ge(pair_used, part.unit(n, 2 * STEPS, 2 * s - 1 + pr))
                for a in range(2):
                    last = pe.matmul(ps[:, B_PAIR + 2 * pr + a, :], qa[:, n % 2, 2 * pr + a, t * P:(t + 1) * P],
                                     kb[:, 2 * (n % QUADS) + pr, j * CW:(j + 1) * CW], start=True, stop=True)
                last.then_inc(pair_s, 1)

            def sums(part, n, kt):
                g = n % QUADS
                if kt == 0 and n >= 1:
                    pe.wait_ge(ot_s, part.unit(n, 1, 0))
                pe.wait_ge(ring_used, part.ring(("scores", n, kt, HQ - 1)))
                for h in range(HQ):
                    j = (n * STEPS + kt) * HQ + h
                    last = pe.matmul(ps[32 * h:32 * h + 32, B_OUT, :], vt[:, kt, HQ * g + h, :],
                                     probs[:, j % PROBS, :], start=(kt == 0), stop=(kt == STEPS - 1))
                last.then_inc(pv_s, 1)

            def turn_sums(part, n, pairs):
                pe.wait_ge(ot_s, part.unit(n, 1, 1))
                pe.wait_ge(pair_used, pairs)
                for t in range(TPC):
                    last = pe.transpose(ps[:, B_PAIR, t * P:(t + 1) * P], ot[:, n % 2, t * P:(t + 1) * P], ident)
                last.then_inc(on_s, 1)

            def step(part, n, kt):
                a = part.a_step(n, kt)

                def maximum(pr):
                    if a is None:
                        return
                    if pr == 0:
                        if kt == SUMS_STEP + 1 and n >= 1:
                            pe.wait_ge(attn_s, part.unit(n, 1, 0))
                        if kt == PROJ_STEP + 1 and n >= 1 and n % QUADS == 0:
                            pe.wait_ge(x1_s, part.unit(n, 1, 0) // QUADS)
                        if a[1] == 0:
                            key = ("queries", a[0], 1)
                            pe.wait_ge(ring_used, part.ring(key) if key in part.items else 4)
                    max_scores(part, *a, pr)

                def scores(heads):
                    for h in heads:
                        key = ("scores", n, kt, h)
                        pe.wait_ge(ring_used, part.ring(key, 1 - SCORE_BANKS))
                        rows = slice(SL * (h % 2), SL * (h % 2) + SL)
                        pe.matmul(ps[:, part.bank(key), :], kb[rows, 2 * (n % QUADS) + h // 2, kt * P:(kt + 1) * P],
                                  qb[rows, n % 2, h // 2, :], start=True, stop=True).then_inc(ring_s, 1)

                late = kt in (SUMS_STEP + 1, PROJ_STEP + 1)
                if not late:
                    maximum(0)
                if kt == ATT_STEP and n >= 1 and n % QUADS == 0:
                    turn_attn(part, n)
                if kt in QUERY_STEPS and part.more(n, 2):
                    turn_q(part, ("queries", n + 2, QUERY_STEPS.index(kt)))
                if kt == STACK_STEP and part.more(n, 1):
                    pe.wait_ge(max_s, part.unit(n, 1, 2))
                    turn_q(part, ("stack", n + 1, 0))
                scores((0, 1))
                maximum(0 if late else 1)
                scores((2, 3))
                if kt >= 1:
                    sums(part, n, kt - 1)
                elif n > part.first:
                    sums(part, n - 1, STEPS - 1)
                elif n >= 1:
                    carried_sums(part, n)
                if late:
                    maximum(1)
                if kt == SUMS_STEP and n >= 1:
                    turn_sums(part, n - 1, part.unit(n, 2 * STEPS, 2 * (kt + LEAD) + 1) if a else 2 * UNITS * STEPS)
                if kt == PROJ_STEP and n >= 1 and n % QUADS == 0:
                    project(part, n)
                if kt == STACK_STEP and part.more(n, 1):
                    turn_q(part, ("stack", n + 1, 1))

            def carried_sums(part, n):
                g = (n - 1) % QUADS
                pe.wait_ge(ring_used, part.ring(("scores", n, 0, 0), 0))
                for h in range(HQ):
                    j = ((n - 1) * STEPS + STEPS - 1) * HQ + h
                    last = pe.matmul(ps[32 * h:32 * h + 32, B_OUT, :], vt[:, STEPS - 1, HQ * g + h, :],
                                     probs[:, j % PROBS, :], start=False, stop=True)
                last.then_inc(pv_s, 1)

            def turn_attn(part, n):
                pe.wait_ge(attn_s, part.unit(n, 1, 0))
                for t in range(TPC):
                    pe.wait_ge(ring_used, part.ring(("att", n, t), 1 - SCORE_BANKS))
                    pe.transpose(ps[:, part.bank(("att", n, t)), 0:P], attn[:, t, :], ident).then_inc(ring_s, 1)

            def project(part, n):
                pe.wait_ge(ring_used, part.ring(("att", n, TPC - 1)))
                pe.wait_ge(pair_used, part.unit(n, 2 * STEPS, 2 * (PROJ_STEP + LEAD) + 1))
                for t in range(TPC):
                    last = pe.matmul(ps[:, B_PAIR, t * P:(t + 1) * P], attT[:, t * P:(t + 1) * P], wcol("proj"),
                                     start=True, stop=True)
                last.then_inc(proj_s, 1)

            start = before()
            pe.wait_ge(kt_used, 4 * CHUNKS)
            for n in range(2):
                for a in range(2):
                    turn_q(start, ("queries", n, a))
            pe.wait_ge(qkv_used, NT)
            for s in range(LEAD):
                if s % STEPS == 0:
                    pe.wait_ge(ring_used, 2 * (s // STEPS) + 2)
                for pr in range(2):
                    max_scores(start, s // STEPS, s % STEPS, pr)
            pe.wait_ge(max_s, 1)
            for a in range(2):
                turn_q(start, ("stack", 0, a))
            pe.wait_ge(pads_s, 2)
            pe.wait_ge(w2_s, 16)
            pe.wait_ge(ring_used, RING0)
            end = attention(pe, step)
            sums(end, UNITS - 1, STEPS - 1)
            pe.wait_ge(attn_s, UNITS - 1)
            turn_sums(end, UNITS - 1, 2 * UNITS * STEPS)
            pe.wait_ge(attn_s, UNITS)
            for t in range(TPC):
                last = pe.transpose(ps[:, B_RING, t * P:(t + 1) * P], attn[:, t, :], ident)
            last.then_inc(on_s, 1)
            pe.wait_ge(ot_s, UNITS + 1)
            for t in range(TPC):
                last = pe.matmul(ps[:, B_PAIR, t * P:(t + 1) * P], attT[:, t * P:(t + 1) * P], wcol("proj"),
                                 start=True, stop=True)
            last.then_inc(proj_s, 1)

            def natural(bank, groups, width=P):
                for t in range(TPC):
                    for m, (z, at, wt) in enumerate(groups):
                        last = pe.matmul(ps[:, bank, t * width:(t + 1) * width], z[:, at + t * P:at + (t + 1) * P],
                                         wt, start=(m == 0), stop=(m == len(groups) - 1))
                return last

            def ffn_rk(s, ht, i):
                q = CHUNKS * s + i
                b = 3 * (i % 2)
                pe.wait_ge(ht_s, CHUNKS * (1 + 2 * s) + i + 1)
                if q >= 2:
                    pe.wait_ge(ks_s, q - 1)
                natural(b, ((ht, 1 + i * CW, wmix[:, 0, :]), (ht, i * CW, wmix[:, 1, :]))).then_inc(r_s, 1)
                pe.matmul(ps[:, b + 1, :], wmix[:, 2, :], ht[:, 1 + i * CW:1 + (i + 1) * CW], start=True, stop=False)
                pe.matmul(ps[:, b + 1, :], wmix[:, 3, :], ht[:, i * CW:(i + 1) * CW], start=False,
                          stop=True).then_inc(kk_s, 1)

            def ffn_v(s, i):
                q = CHUNKS * s + i
                pe.wait_ge(ks_s, q + 1)
                if q >= 2:
                    pe.wait_ge(xf_s, q - 1)
                natural(2 + 3 * (i % 2), ((ks[:, i % 2, :], 0, wcol("v")),)).then_inc(v_s, 1)

            pe.wait_ge(mix_s, 1)
            pe.wait_ge(x1_s, CHUNKS)
            for i in range(CHUNKS + 2):
                if i < CHUNKS:
                    turn_xn(CHUNKS + i)
                if 1 <= i <= CHUNKS:
                    ffn_rk(0, ht1, i - 1)
                if i >= 2:
                    ffn_v(0, i - 2)
            pe.wait_ge(xf_s, CHUNKS)
            for i in range(CHUNKS + 2):
                if i < CHUNKS:
                    turn_xn(2 * CHUNKS + i)
                if 1 <= i <= CHUNKS:
                    j = i - 1
                    pe.wait_ge(ht_s, 2 * CHUNKS + j + 1)
                    if j >= 1:
                        pe.wait_ge(kv3a_s, j)
                    pe.matmul(ps[:, 0, :], wcol("lin_qkv", 0, C), ht0[:, 1 + j * CW:1 + (j + 1) * CW],
                              start=True, stop=True).then_inc(q3_s, 1)
                    for t in range(TPC):
                        last = pe.matmul(ps[:, 1 + t // 2, (t % 2) * 2 * C:(t % 2 + 1) * 2 * C],
                                         ht0[:, 1 + j * CW + t * P:1 + j * CW + (t + 1) * P],
                                         wcol("lin_qkv", C, 3 * C), start=True, stop=True)
                    last.then_inc(kv3_s, 1)
                if i >= 2:
                    j = i - 2
                    pe.wait_ge(kv3a_s, j + 1)
                    for t in range(TPC):
                        last = pe.matmul(ps[:, 3, 0:C + 1], kn3[:, j % 2, t, :], vn3[:, j % 2, t, 0:C + 1],
                                         start=(j == 0 and t == 0), stop=(j == CHUNKS - 1 and t == TPC - 1))
                    last.then_inc(ctx_s, 1)
            pe.wait_ge(ctxm_s, 1)

            def lin_out(i):
                if i >= 1:
                    pe.wait_ge(ln_s, i)
                for t in range(TPC):
                    last = pe.matmul(ps[:, t // 2, (t % 2) * 256:(t % 2) * 256 + C + H],
                                     qt[:, i * CW + t * P:i * CW + (t + 1) * P], ctxm, start=True, stop=True)
                last.then_inc(lo_s, 1)

            def lin_turn(i):
                pe.wait_ge(ln_s, i + 1)
                if i >= 2:
                    pe.wait_ge(lta_s, i - 1)
                for t in range(TPC):
                    last = pe.transpose(ps[:, 4 + i % 2, t * P:(t + 1) * P], at3[:, i % 2, t, :], ident)
                last.then_inc(lt_s, 1)

            def lin_proj(i):
                pe.wait_ge(lta_s, i + 1)
                if i >= 1:
                    pe.wait_ge(lx_s, i)
                natural(6, ((att3[:, i % 2, :], 0, wcol("lin_proj")),)).then_inc(lp_s, 1)

            pe.wait_ge(q3a_s, CHUNKS)
            lin_out(0)
            for i in range(CHUNKS):
                lin_turn(i)
                if i + 1 < CHUNKS:
                    lin_out(i + 1)
                lin_proj(i)
                if i >= 1:
                    turn_xn(3 * CHUNKS + i - 1)
            turn_xn(4 * CHUNKS - 1)
            for i in range(CHUNKS + 1):
                if i < CHUNKS:
                    ffn_rk(1, ht1, i)
                if i >= 1:
                    ffn_v(1, i - 1)

        @block.vector
        def _(dve):
            links = [0]

            def link(ins):
                links[0] += 1
                ins.then_inc(chain, 1)
                dve.wait_ge(chain, links[0])

            dve.wait_ge(k_s, 16)
            dve.tensor_copy(identb[:, :], ident).then_inc(identb_s, 1)

            def ln_stats(q, i):
                if q >= 1:
                    dve.wait_ge(stats_s, q)
                if q >= 2:
                    dve.wait_ge(xn_s, q - 1)
                for t in range(TPC):
                    ins = dve.bn_stats(stats[:, t, :], x[:, i * TPC + t, :])
                link(ins)
                for t in range(TPC):
                    ins = dve.bn_aggr(mv[:, q % 2, t, :], stats[:, t, :])
                ins.then_inc(stats_s, 1)

            def ln_apply(q, i):
                dve.wait_ge(rstd_s, q + 1)
                dve.wait_ge(stats_s, q + 1)
                if q >= 2:
                    dve.wait_ge(xt_s, q - 1)
                for t in range(TPC):
                    ins = dve.tensor_scalar(xn[:, q % 2, t, :], x[:, i * TPC + t, :], mv[:, q % 2, t, 0:1],
                                            rstd[:, q % 2, t:t + 1], ALU.subtract, ALU.mult)
                ins.then_inc(xn_s, 1)

            def qkv_store(i):
                if i == 0:
                    dve.wait_ge(w1_s, 16)
                for t in range(TPC):
                    tile = i * TPC + t
                    dve.wait_ge(qkv_s, tile + 1)
                    dve.tensor_tensor(qk[:, t, :], ps[:, t, 0:2 * C], wcol("qkv_b", 0, 2 * C), ALU.add)
                    ins = dve.tensor_tensor(vt[:, tile, :, 0:D], ps[:, t, 2 * C:3 * C].rearrange("p (h d) -> p h d", h=H),
                                            wcol("qkv_b", 2 * C, 3 * C).rearrange("p (h d) -> p h d", h=H), ALU.add)
                    ins.then_inc(qkv_used, 1)
                dve.wait_ge(qkv_used, (i + 1) * TPC)

            def rope(i):
                v = qk.rearrange("p t (g j two) -> p t g j two", g=2 * H, two=2)
                r = rot.rearrange("p t (g j two) -> p t g j two", g=2 * H, two=2)
                e, od = v[:, :, :, :, 0], v[:, :, :, :, 1]
                m = tmp.rearrange("p t (two g j) -> p t g j two", two=2, g=2 * H)
                m0, m1 = m[:, :, :, :, 0], m[:, :, :, :, 1]
                tt = slice(i * TPC, (i + 1) * TPC)
                cs = cos[:, tt, :].unsqueeze(2).broadcast_to([P, TPC, 2 * H, D // 2])
                sn = sin[:, tt, :].unsqueeze(2).broadcast_to([P, TPC, 2 * H, D // 2])
                dve.tensor_tensor(m0, od, sn, ALU.mult)
                dve.tensor_tensor(m1, od, cs, ALU.mult)
                dve.tensor_tensor(r[:, :, :, :, 0], e, cs, ALU.mult)
                link(dve.tensor_tensor(r[:, :, :, :, 1], e, sn, ALU.mult))
                dve.tensor_tensor(r[:, :, :, :, 0], r[:, :, :, :, 0], m0, ALU.subtract)
                link(dve.tensor_tensor(r[:, :, :, :, 1], r[:, :, :, :, 1], m1, ALU.add))

            def split(i):
                t = slice(i * TPC, (i + 1) * TPC)
                r = rot.rearrange("p t (z h d) -> p t z h d", z=2, h=H)
                q, k, qs, ks_ = r[:, :, 0], r[:, :, 1], qn[:, t], kn[:, t]
                dve.tensor_copy(qs[:, :, :, 0:D], q)
                link(dve.tensor_copy(ks_[:, :, :, 0:D], k))
                dve.tensor_tensor(q, q, qs[:, :, :, 0:D], ALU.subtract)
                link(dve.tensor_tensor(k, k, ks_[:, :, :, 0:D], ALU.subtract))
                dve.tensor_copy(qs[:, :, :, 16:16 + D], q)
                link(dve.tensor_copy(ks_[:, :, :, 8:8 + D], k))
                dve.tensor_tensor(qs[:, :, :, S_C + 8:S_C + 8 + D], q, qs[:, :, :, 16:16 + D], ALU.subtract)
                dve.tensor_tensor(ks_[:, :, :, S_C:S_C + D], k, ks_[:, :, :, 8:8 + D], ALU.subtract).then_inc(split_s, 1)

            def take_x(i):
                dve.wait_ge(x_in_s[i], 16)
                ln_stats(i, i)

            take_x(0)
            for i in range(CHUNKS):
                ln_apply(i, i)
                if i + 1 < CHUNKS:
                    take_x(i + 1)
                qkv_store(i)
                rope(i)
                split(i)
            dve.wait_ge(w2_s, 16)
            pb = wcol("proj_b").unsqueeze(1).broadcast_to([P, NT, C])
            link(dve.tensor_tensor(x[:, :, :], x[:, :, :], pb, ALU.add))

            def take_max(part, n, s):
                t, j = divmod(s, TPC)
                for pr in range(2):
                    dve.wait_ge(pair_s, part.unit(n, 2 * STEPS, 2 * s + pr + 1))
                    dve.tensor_reduce(mpart[:, n % 2, t, 2 * pr:2 * pr + 2, j],
                                      ps[:, B_PAIR + 2 * pr:B_PAIR + 2 * pr + 2, :],
                                      AX.X, ALU.max).then_inc(pair_used, 1)

            LINKS_PER_UNIT = 3

            def put_max(part, n):
                g = n % QUADS
                before_ = part.unit(n, LINKS_PER_UNIT, links[0] - (1 if n else 0))
                dve.wait_ge(pair_used, part.unit(n, 2 * STEPS, 2 * STEPS))
                dve.tensor_reduce(negm[:, :, :], mpart[:, n % 2], AX.X, ALU.max, negate=True).then_inc(chain, 1)
                dve.wait_ge(chain, before_ + 1)
                tiles = bass.ds(part.chunk_tile(n, 0), TPC)
                slot = qn[:, tiles, HQ * g:HQ * g + HQ, S_MAX]
                dve.tensor_copy(slot, negm[:, :, :]).then_inc(chain, 1)
                dve.wait_ge(chain, before_ + 2)
                dve.tensor_tensor(qn[:, tiles, HQ * g:HQ * g + HQ, S_MAX + 1], negm[:, :, :], slot,
                                  ALU.subtract).then_inc(max_s, 1)

            def scale_sums(part, n):
                g = n % QUADS
                dve.wait_ge(on_s, part.unit(n, 1, 1))
                v = ps[:, B_PAIR, :].rearrange("p (t h s) -> p t h s", t=TPC, h=HQ)
                dve.reciprocal(rsum[:, :, :], v[:, :, :, D]).then_inc(chain, 1)
                ahead = min(n + 2, UNITS) if not part.per else None
                if ahead is not None:
                    dve.wait_ge(chain, links[0] + 2 * ahead + n + 1)
                else:
                    dve.wait_ge(chain, part.unit(n, LINKS_PER_UNIT, links[0] + 5))
                out_ = attn[:, :, 32 * g:32 * g + 32].rearrange(
                    "p t (h d) -> p t h d", h=HQ)
                dve.tensor_tensor(out_, v[:, :, :, 0:D], rsum[:, :, :].unsqueeze(3).broadcast_to([P, TPC, HQ, D]),
                                  ALU.mult).then_inc(attn_s, 1)

            def add_proj(part, n):
                dve.wait_ge(proj_s, part.unit(n, 1, 0) // QUADS if part.per else n // QUADS)
                tiles = x[:, bass.ds(part.chunk_tile(n, -TPC), TPC), :]
                dve.tensor_tensor(tiles, tiles, ps[:, B_PAIR, :].rearrange("p (t c) -> p t c", t=TPC),
                                  ALU.add).then_inc(x1_s, 1)

            def step(part, n, kt):
                a = part.a_step(n, kt)
                if a is not None:
                    take_max(part, *a)
                    if a[1] == STEPS - 1:
                        put_max(part, a[0])
                if kt == SUMS_STEP and n >= 1:
                    scale_sums(part, n - 1)
                if kt == PROJ_STEP and n >= 1 and n % QUADS == 0:
                    add_proj(part, n)

            start = before()
            for s in range(LEAD):
                take_max(start, s // STEPS, s % STEPS)
                if s % STEPS == STEPS - 1:
                    put_max(start, s // STEPS)
            end = attention(dve, step)
            scale_sums(end, UNITS - 1)
            links[0] += 3 * UNITS
            dve.wait_ge(proj_s, CHUNKS)
            tiles = x[:, NT - TPC:NT, :]
            dve.tensor_tensor(tiles, tiles, ps[:, B_PAIR, :].rearrange("p (t c) -> p t c", t=TPC),
                              ALU.add).then_inc(x1_s, 1)
            dve.wait_ge(x1_s, CHUNKS)

            link(dve.tensor_scalar(onem, wcol("mu"), -1.0, 1.0, ALU.mult, ALU.add))
            for m, name in enumerate(("r", "k")):
                dve.tensor_scalar(wmix[:, 2 * m, :], wcol(name), wcol("mu", m, m + 1), None, ALU.mult)
                dve.tensor_scalar(wmix[:, 2 * m + 1, :], wcol(name), onem[:, m:m + 1], None, ALU.mult)
            dve.memset(ht1[:, 0:1], 0.0)
            dve.memset(vn3[:, :, :, C:C + 1], 1.0)
            dve.memset(ht0[:, 0:1], 0.0).then_inc(mix_s, 1)

            def ffn_add(s, i):
                q = CHUNKS * s + i
                t = slice(i * TPC, (i + 1) * TPC)
                dve.wait_ge(sg_s, q + 1)
                dve.wait_ge(v_s, q + 1)
                link(dve.tensor_tensor(vs, ps[:, 2 + 3 * (i % 2), :], sg[:, i % 2, :], ALU.mult))
                dve.tensor_tensor(x[:, t, :], x[:, t, :], vs.rearrange("p (t c) -> p t c", t=TPC),
                                  ALU.add).then_inc(xf_s, 1)
                dve.wait_ge(xf_s, q + 1)

            ln_stats(CHUNKS, 0)
            for i in range(CHUNKS):
                if i + 1 < CHUNKS:
                    ln_stats(CHUNKS + i + 1, i + 1)
                ln_apply(CHUNKS + i, i)
            for i in range(CHUNKS + 1):
                if i < CHUNKS:
                    ffn_add(0, i)
                    ln_stats(2 * CHUNKS + i, i)
                if i >= 1:
                    ln_apply(2 * CHUNKS + i - 1, i - 1)
            pb3 = wcol("lin_proj_b").unsqueeze(1).broadcast_to([P, NT, C])
            dve.wait_ge(xn_s, 3 * CHUNKS)
            link(dve.tensor_tensor(x[:, :, :], x[:, :, :], pb3, ALU.add))
            dve.wait_ge(ctx_s, CHUNKS)
            dve.tensor_tensor(ctxm[:, 0:C], block_mask, ps[:, 3, 0:C], ALU.mult)
            link(dve.tensor_copy(ksum, ps[:, 3, C:C + 1]))
            heads = block_mask.rearrange("p (h d) -> p h d", h=H)[:, :, 0]
            dve.tensor_scalar(ctxm[:, C:C + H], heads, ksum, None, ALU.mult).then_inc(ctxm_s, 1)

            def lin_scale(i):
                dve.wait_ge(lo_s, i + 1)
                if i >= 2:
                    dve.wait_ge(lt_s, i - 1)
                v = ps[:, 0:2, :].rearrange("p b (t c) -> p (b t) c", t=2)
                link(dve.tensor_scalar(zz[:, 0], v[:, :, C:C + H], Z_EPS, None, ALU.add))
                link(dve.reciprocal(zz[:, 1], zz[:, 0]))
                dve.tensor_tensor(at3[:, i % 2].rearrange("p t (h d) -> p t h d", h=H),
                                  v[:, :, 0:C].rearrange("p t (h d) -> p t h d", h=H),
                                  zz[:, 1].unsqueeze(3).broadcast_to([P, TPC, H, D]), ALU.mult).then_inc(ln_s, 1)

            def lin_add(i):
                t = slice(i * TPC, (i + 1) * TPC)
                dve.wait_ge(lp_s, i + 1)
                dve.tensor_tensor(x[:, t, :], x[:, t, :], ps[:, 6, :].rearrange("p (t c) -> p t c", t=TPC),
                                  ALU.add).then_inc(lx_s, 1)
                dve.wait_ge(lx_s, i + 1)
                ln_stats(3 * CHUNKS + i, i)

            lin_scale(0)
            for i in range(CHUNKS):
                if i + 1 < CHUNKS:
                    lin_scale(i + 1)
                lin_add(i)
                ln_apply(3 * CHUNKS + i, i)
            for i in range(CHUNKS):
                ffn_add(1, i)


def rope_tables():
    import numpy as np
    inv = (np.float32(1.0) / np.float32(10000.0) ** (np.arange(0, D, 2, dtype=np.float32) / np.float32(D))).astype(np.float32)
    freqs = (np.arange(N, dtype=np.float32)[:, None] * inv[None, :]).astype(np.float32)

    def lay(z):
        return z.astype(np.float32).reshape(NT, P, D // 2).transpose(1, 0, 2).reshape(P, NT * D // 2)
    return lay(np.cos(freqs.astype(np.float64))), lay(np.sin(freqs.astype(np.float64)))


def kernel(**inputs):
    import numpy as np
    import concourse.bacc as bacc
    from concourse.bass_utils import run_bass_kernel_spmd

    g = {k: np.asarray(v) for k, v in inputs.items()}

    def rows(v):
        return np.broadcast_to(v[None, :], (P, v.shape[0]))

    parts = {
        "qkv": g["L0_attn_a_qkv_w"].T, "qkv_b": rows(g["L0_attn_a_qkv_b"]), "proj": g["L0_attn_a_proj_w"].T,
        "proj_b": rows(g["L0_attn_a_proj_b"]), "lin_qkv": g["L0_attn_b_w_qkv"].T, "lin_proj": g["L0_attn_b_w_proj"].T,
        "lin_proj_b": rows(g["L0_attn_b_b_proj"]), "r": g["L0_ffn_W_r"].T, "k": g["L0_ffn_W_k"].T,
        "v": g["L0_ffn_W_v"].T, "mu": np.stack([g["L0_ffn_mu_r"], g["L0_ffn_mu_k"]], axis=1),
    }
    weights = np.ascontiguousarray(np.concatenate([parts[n] for n in W_COLS], axis=1))
    cos, sin = rope_tables()
    head = np.arange(P) // D
    consts = np.ascontiguousarray(np.concatenate(
        [cos, sin, np.eye(P, dtype=np.float32), (head[:, None] == head[None, :]).astype(np.float32)], axis=1))
    xs = np.ascontiguousarray(g["L0_attn_a_x"].reshape(N, C))

    nc = bacc.Bacc("TRN2", target_bir_lowering=False, num_devices=1)
    arrays = {"x_dram": xs, "w_dram": weights, "k_dram": consts}
    args = [nc.dram_tensor(n, a.shape, mybir.dt.from_np(a.dtype), kind="ExternalInput").ap() for n, a in arrays.items()]
    out = nc.dram_tensor("out_dram", (N, C), F32, kind="ExternalOutput").ap()
    build(nc, *args, out)
    r = run_bass_kernel_spmd(nc, [arrays], core_ids=[0])
    return r.results[0]["out_dram"].reshape(1, N, C)
```

```python
from contextlib import ExitStack

import concourse.bass as bass
from concourse import mybir

ALU = mybir.AluOpType
ACT = mybir.ActivationFunctionType
AX = mybir.AxisListType
F32 = mybir.dt.float32
BF16 = mybir.dt.bfloat16

P = 128
N = 2048
C = 128
H = 16
D = C // H
NT = N // P
CHUNKS = 4
TPC = NT // CHUNKS
CW = N // CHUNKS
QUADS = 4
HQ = H // QUADS
UNITS = CHUNKS * QUADS
STEPS = NT
LN_EPS = 1e-5
Z_EPS = 2.0 ** -23
SCALE = float(D) ** -0.5

SL = 64
S_MAX = 32
S_C = 40

SCORE_BANKS = 3
PROBS = 8
LEAD = STEPS + 2

SUMS_STEP = 2
ATT_STEP = 5
PROJ_STEP = 7
QUERY_STEPS = (9, 11)
STACK_STEPS = (14, 15)

LATE_PE = {-1: [("ht", 0)], 0: [("ht", 1)], 1: [("rk", 0)], 2: [("v", 0), ("ht", 2)], 3: [("rk", 1)], 4: [("v", 1)],
           5: [("ht3", 0)], 6: [("rk", 2)], 7: [("v", 2)], 9: [("qkv3", 0)], 11: [("ht3", 1)], 12: [("ht3", 2)]}
LATE_ACT = {-1: [("ht", 0)], 0: [("ht", 1)], 1: [("gate", 0)], 2: [("ht", 2)], 3: [("gate", 1)],
            5: [("ht3", 0)], 6: [("gate", 2)], 11: [("ht3", 1)], 12: [("ht3", 2)]}
LATE_DVE = {-3: [("stats", 4), ("apply", 4)], -2: [("stats", 5), ("apply", 5)],
            -1: [("constants", 0), ("mix", 0), ("stats", 6)], 0: [("mix", 1), ("apply", 6)], 1: [("square", 0)],
            2: [("add", 0), ("stats", 7)], 3: [("mix", 2), ("square", 1), ("apply", 7)], 4: [("add", 1), ("stats", 8)],
            6: [("square", 2), ("apply", 8)], 7: [("add", 2), ("stats", 9)], 9: [("apply", 9), ("qkv3", 0)]}
QKV3 = {i: "kvq" for i in range(CHUNKS)}
QKV3[CHUNKS - 2] = "kqv"
NORMS = [(0, i) for i in range(CHUNKS)] + [(which, i) for which in (1, 2) for i in range(CHUNKS - 1)]
NORMS += [(1, CHUNKS - 1), (2, CHUNKS - 1)] + [(3, i) for i in range(CHUNKS)]

ACT_NORMS = (0, 3)

POOL_K = 2
DVE_K = CHUNKS - POOL_K

B_PAIR = 0
B_RING = 4
B_OUT = 7
B_XT = 2
B_K, B_Q, B_V = 4, 5, 6
B_HT, B_R, B_KV, B_CTX = 0, 1, 2, 3

W_COLS = {}
for _name, _n in (("qkv", 3 * C), ("qkv_b", 3 * C), ("proj", C), ("proj_b", C), ("lin_qkv", 3 * C), ("lin_proj", C),
                  ("lin_proj_b", C), ("r", C), ("k", C), ("v", C), ("mu", 2)):
    W_COLS[_name] = (sum(n for _, n in W_COLS.values()), _n)
W_TOTAL = sum(n for _, n in W_COLS.values())
W_FIRST = 6 * C
K_COS, K_SIN, K_IDENT, K_BLOCK, K_TOTAL = 0, 64, 128, 256, 384


def beside(n, kt):
    if kt == SUMS_STEP and n > 0 and n % 2 == 0:
        return [("sums", n // 2 - 1)]
    if kt == ATT_STEP and n % QUADS == 0 and n > 0:
        return [("att", n)]
    if kt == PROJ_STEP and n % QUADS == 0 and n > 0:
        return [("proj", n)]
    if kt in QUERY_STEPS and n + 2 < UNITS:
        return [("queries", n + 2, QUERY_STEPS.index(kt))]
    if kt in STACK_STEPS and n + 1 < UNITS:
        return [("stack", n + 1, STACK_STEPS.index(kt))]
    return []


LAST_ITEM = ("att", UNITS)


def ring_places(first, last):
    keys = []
    for n in range(first, last + 1):
        for kt in range(STEPS):
            keys += [("scores", n, kt, h) for h in range(HQ)] + beside(n, kt)
    if last == UNITS - 1:
        keys.append(LAST_ITEM)
    return {key: i for i, key in enumerate(keys)}, len(keys)


def build(nc, x_in, w_in, k_in, out):
    ctx = ExitStack()
    with ctx:
        def sb(name, shape, dt):
            return ctx.enter_context(nc.sbuf_tensor(name, shape, dt))

        def sem(name):
            return ctx.enter_context(nc.semaphore(name))

        ps = ctx.enter_context(nc.psum_tensor("ps", [P, 8, 512], F32))
        w = sb("w", [P, W_TOTAL], F32)
        kc = sb("kc", [P, K_TOTAL], F32)
        identb = sb("identb", [P, P], BF16)
        x = sb("x", [P, NT, C], F32)
        stats = sb("stats", [P, TPC, 6], F32)
        mv = sb("mv", [P, CHUNKS, TPC, 2], F32)
        ve = sb("ve", [P, TPC], F32)
        neghalf = sb("neghalf", [P, TPC], F32)
        rstd = sb("rstd", [P, CHUNKS, TPC], F32)
        shift = sb("shift", [P, CHUNKS, TPC], F32)
        xn = sb("xn", [P, 2, TPC, C], F32)
        ht0 = sb("ht0", [P, N + 1], F32)
        kb = sb("kb", [P, H // 2, N], BF16)
        vt = sb("vt", [P, NT, H, 32], F32)
        qa = sb("qa", [P, 2, HQ, CW], BF16)
        qb = sb("qb", [P, 2, 2, CW], BF16)
        mpart = sb("mpart", [P, 2, TPC, HQ, TPC], F32)
        negm = sb("negm", [P, TPC, HQ], F32)
        rsum = sb("rsum", [P, TPC, HQ, 2], F32)
        qn_raw = sb("qn_raw", [P, NT * H * SL // 2], F32)
        kn_raw = sb("kn_raw", [P, NT * H * SL // 2], F32)
        first = sb("first", [P, 4 + CHUNKS + POOL_K, TPC, C], F32)

        qn = qn_raw[:, :].bitcast(BF16).rearrange("p (t h s) -> p t h s", t=NT, h=H)
        kn = kn_raw[:, :].bitcast(BF16).rearrange("p (t h s) -> p t h s", t=NT, h=H)
        kn_rows = kn_raw[:, :].bitcast(BF16).rearrange("p (t s) -> p t s", t=NT)
        qn_rows = qn_raw[:, :].bitcast(BF16).rearrange("p (t s) -> p t s", t=NT)
        kraw, krot, ktmp, qtmp = (first[:, m] for m in range(4))
        qraw, kraw_pool = first[:, 4:4 + CHUNKS], first[:, 4 + CHUNKS:]
        probs = kn_raw[:, 0:PROBS * 512].rearrange("p (b n) -> p b n", b=PROBS)
        at = PROBS * 512
        ot = kn_raw[:, at:at + 2 * 512].rearrange("p (b n) -> p b n", b=2)
        at += 2 * 512
        attn = kn_raw[:, at:at + CW].rearrange("p (t c) -> p t c", t=TPC)
        at += CW
        attT = kn_raw[:, at:at + CW]
        at += CW
        turned = kn_raw[:, at:at + 512]
        at += 512
        proj = kn_raw[:, at:at + CW]

        def wcol(name, a=0, b=None):
            at, n = W_COLS[name]
            return w[:, at + a:at + (n if b is None else b)]

        ident = kc[:, K_IDENT:K_IDENT + P]
        cos = kc[:, K_COS:K_COS + 64].rearrange("p (t i) -> p t i", t=NT)
        sin = kc[:, K_SIN:K_SIN + 64].rearrange("p (t i) -> p t i", t=NT)
        block_mask = kc[:, K_BLOCK:K_BLOCK + P]

        ht1 = qn_raw[:, 0:N + 1]
        qt = qn_raw[:, N + 4:2 * N + 4]
        o = 2 * N + 4
        sg = qn_raw[:, o:o + 1024].rearrange("p (b n) -> p b n", b=2)
        ks = qn_raw[:, o + 1024:o + 2048].rearrange("p (b n) -> p b n", b=2)
        kr = qn_raw[:, o + 2048:o + 2560]
        xr = qn_raw[:, o + 2560:o + 3584].rearrange("p (b n) -> p b n", b=2)
        at += CW
        vs = kn_raw[:, at:at + 512]
        diff = kn_raw[:, at + 512:at + 1024]
        late = first.rearrange("p a t c -> p (a t c)")
        kn3 = late[:, 0:1024].rearrange("p (b t c) -> p b t c", b=2, t=TPC)
        vn3 = late[:, 1024:1024 + 2 * TPC * 132].rearrange("p (b t c) -> p b t c", b=2, t=TPC)
        o = 1024 + 2 * TPC * 132
        xk = late[:, o:o + 1024].rearrange("p (b n) -> p b n", b=2)
        at3 = kn_raw[:, 0:1024].rearrange("p (b t c) -> p b t c", b=2, t=TPC)
        att3 = kn_raw[:, 1024:2048].rearrange("p (b n) -> p b n", b=2)
        zz = kn_raw[:, 2048:2048 + 2 * TPC * H].rearrange("p (a t h) -> p a t h", a=2, t=TPC)
        ctxm = kn_raw[:, 2200:2200 + C + H]
        ksum = kn_raw[:, 2400:2401]

        x_in_s = [sem(f"x_loaded{i}") for i in range(CHUNKS)]
        w1_s, w2_s, k_s = sem("first_weights_loaded"), sem("other_weights_loaded"), sem("constants_loaded")
        identb_s = sem("identb_ready")
        pads_s = sem("pads_ready")
        stats_s = sem("ln_stats_ready")
        pool_chain = sem("pool_chain")
        rstd_s = sem("rstd_ready")
        xn_s = sem("xn_ready")
        xt_s = sem("xn_turned")
        ht_s = sem("ht_ready")
        k_mm = sem("k_products_ready")
        qv_mm = sem("qv_products_ready")
        k_taken = sem("k_taken")
        qv_taken = sem("qv_taken")
        split_s = sem("k_split")
        dups_s = sem("k_repeated")
        q_split = sem("q_split")
        values_s = sem("values_ready")
        q0t_s = sem("first_queries_turned")
        q0_s = sem("first_queries_stored")
        xb_s = sem("x_with_proj_bias")
        turns_begun = sem("turns_begun")
        kt_s = sem("keys_turned")
        kt_used = sem("keys_stored")
        chain = sem("dve_chain")
        late_chain = sem("dve_late_chain")
        pair_s = sem("pair_ready")
        pair_used = sem("pair_used")
        max_s = sem("max_ready")
        ring_s = sem("ring_ready")
        ring_used = sem("ring_used")
        pv_s = sem("sums_step_done")
        ot_s = sem("sums_stored")
        attn_s = sem("attn_ready")
        last_s = sem("last_unit_in_bank")
        x1_s = sem("x1_ready")
        late_s = sem("late_constants_ready")
        mix_s = sem("mixed_ready")
        r_s, kk_s, v_s = sem("r_ready"), sem("k_ready"), sem("v_ready")
        sg_s, kr_s = sem("gate_ready"), sem("relu_ready")
        ks_s = sem("square_ready")
        xf_s = sem("ffn_added")
        q3_s, kv3_s = sem("lin_q_ready"), sem("lin_kv_ready")
        q3a_s, kv3a_s = sem("lin_q_stored"), sem("lin_kv_stored")
        ctx_s = sem("context_ready")
        ctxm_s = sem("context_masked")
        lo_s = sem("lin_out_ready")
        ln_s = sem("lin_out_scaled")
        lt_s = sem("lin_out_turned")
        lta_s = sem("lin_out_stored")
        lp_s = sem("lin_proj_ready")
        lx_s = sem("lin_added")
        out_s = sem("out_written")

        block = ctx.enter_context(nc.Block())

        head_items, head_n = ring_places(0, 0)
        body_items, body_n = ring_places(1, QUADS)
        tail_items, _ = ring_places(3 * QUADS + 1, UNITS - 1)
        start_keys = [("keys", g, i) for g in range(1, QUADS) for i in range(CHUNKS - 1)]
        EARLY = len(start_keys)
        start_keys += [("keys", 1, CHUNKS - 1)] + [("queries", 1, a) for a in range(2)]
        start_keys += [("keys", g, CHUNKS - 1) for g in range(2, QUADS)] + [("stack", 0, a) for a in range(2)]
        RING0 = len(start_keys)
        assert body_n % SCORE_BANKS == 0

        class Part:

            def __init__(self, first, last, items, start, c=0, per_c=0):
                self.first, self.last, self.items, self.start, self.c, self.per = first, last, items, start, c, per_c

            def unit(self, n, times=1, plus=0):
                if self.per:
                    return self.c * (QUADS * times) + (n * times + plus)
                return n * times + plus

            def pair(self, m):
                return self.c * (QUADS // 2) + m if self.per else m

            def ring(self, key, plus=1):
                v = self.start + self.items[key] + plus
                return self.c * self.per + v if self.per else v

            def bank(self, key):
                return B_RING + (self.start + self.items[key]) % SCORE_BANKS

            def a_step(self, n, kt):
                s = n * STEPS + kt + LEAD
                if not self.per and s >= UNITS * STEPS:
                    return None
                return s // STEPS, s % STEPS

            def more(self, n, k):
                return bool(self.per) or n + k < UNITS

            def chunk_tile(self, n, t):
                if self.per:
                    return self.c * TPC + (TPC * (n // QUADS) + t)
                return TPC * (n // QUADS) + t

        def attention(eng, step):
            for n in range(0, 1):
                for kt in range(STEPS):
                    step(Part(0, 0, head_items, RING0), n, kt)
            with eng.Fori(0, CHUNKS - 1) as c:
                part = Part(1, QUADS, body_items, RING0 + head_n, c, body_n)
                for n in range(1, QUADS + 1):
                    for kt in range(STEPS):
                        step(part, n, kt)
            part = last_part()
            for n in range(3 * QUADS + 1, UNITS):
                for kt in range(STEPS):
                    step(part, n, kt)
            return part

        def last_part():
            return Part(3 * QUADS + 1, UNITS - 1, tail_items, RING0 + head_n + (CHUNKS - 1) * body_n)

        def before():
            return Part(0, 0, {key: i for i, key in enumerate(start_keys)}, 0)

        @block.sync
        def _(sp):
            xv = x_in.rearrange("(t p) c -> p t c", p=P)
            ov = out.rearrange("(t p) c -> p t c", p=P)
            sp.dma_start(x[:, 0:TPC, :], xv[:, 0:TPC, :]).then_inc(x_in_s[0], 16)
            sp.dma_start(kc[:, :], k_in).then_inc(k_s, 16)
            sp.dma_start(w[:, 0:W_FIRST], w_in[:, 0:W_FIRST]).then_inc(w1_s, 16)
            for i in range(1, CHUNKS):
                sp.dma_start(x[:, i * TPC:(i + 1) * TPC, :], xv[:, i * TPC:(i + 1) * TPC, :]).then_inc(x_in_s[i], 16)
            sp.dma_start(w[:, W_FIRST:], w_in[:, W_FIRST:]).then_inc(w2_s, 16)
            for i in range(CHUNKS):
                sp.wait_ge(xf_s, CHUNKS + i + 1)
                sp.dma_start(ov[:, i * TPC:(i + 1) * TPC, :], x[:, i * TPC:(i + 1) * TPC, :]).then_inc(out_s, 16)
            sp.wait_ge(out_s, 16 * CHUNKS)

        @block.gpsimd
        def _(pool):
            links = [0]

            def link(ins):
                links[0] += 1
                ins.then_inc(pool_chain, 1)
                pool.wait_ge(pool_chain, links[0])

            def pads(raw):
                words = raw[:, :].rearrange("p (g s) -> p g s", s=SL // 2)
                pool.memset(words[:, :, S_MAX // 2:S_C // 2], 0.0)
                return pool.memset(words[:, :, (S_C + 16) // 2:], 0.0)

            def root(q):
                pool.wait_ge(stats_s, q + 1)
                if q >= 1:
                    pool.wait_ge(rstd_s, q)
                if NORMS[q][0] in ACT_NORMS:
                    pool.tensor_scalar(shift[:, q % CHUNKS, :], mv[:, q % CHUNKS, :, 0], -1.0, None, ALU.mult)
                link(pool.tensor_scalar(ve[:, :], mv[:, q % CHUNKS, :, 1], LN_EPS, None, ALU.add))
                ins = pool.tensor_tensor(rstd[:, q % CHUNKS, :], ve[:, :], neghalf[:, :], ALU.pow)
                if NORMS[q][0] in ACT_NORMS:
                    link(ins)
                    z = shift[:, q % CHUNKS, :]
                    ins = pool.tensor_tensor(z, z, rstd[:, q % CHUNKS, :], ALU.mult)
                ins.then_inc(rstd_s, 1)

            link(pool.memset(neghalf[:, :], -0.5))
            link(pads(kn_raw))
            pool.memset(kn_raw[:, :].bitcast(BF16).rearrange("p (g s) -> p g s", s=SL)[:, :, S_MAX:S_MAX + 2],
                        1.0).then_inc(pads_s, 1)
            for q in range(CHUNKS):
                root(q)
            pads(qn_raw)
            pool.memset(qa[:, 0, :, :].bitcast(F32), 0.0).then_inc(pads_s, 1)

            def rotate(z, i, m):
                bias = wcol("qkv_b", m * C, (m + 1) * C).unsqueeze(1).broadcast_to([P, TPC, C])
                link(pool.tensor_tensor(z, z, bias, ALU.add))
                v = z.rearrange("p t (g j two) -> p t g j two", g=H, two=2)
                e, od = v[:, :, :, :, 0], v[:, :, :, :, 1]
                m = qtmp.rearrange("p t (two g j) -> p t g j two", two=2, g=H)
                m0, m1 = m[:, :, :, :, 0], m[:, :, :, :, 1]
                tt = slice(i * TPC, (i + 1) * TPC)
                cs = cos[:, tt, :].unsqueeze(2).broadcast_to([P, TPC, H, D // 2])
                sn = sin[:, tt, :].unsqueeze(2).broadcast_to([P, TPC, H, D // 2])
                pool.tensor_tensor(m0, od, sn, ALU.mult)
                link(pool.tensor_tensor(m1, od, cs, ALU.mult))
                link(pool.tensor_tensor(od, e, sn, ALU.mult))
                pool.tensor_tensor(od, od, m1, ALU.add)
                link(pool.tensor_tensor(e, e, cs, ALU.mult))
                return pool.tensor_tensor(e, e, m0, ALU.subtract)

            def split(z, to_, first_slots, second_slots, third_slot):
                z = z.rearrange("p t (h d) -> p t h d", h=H)
                for slots in (first_slots, second_slots):
                    for at in slots:
                        ins = pool.tensor_copy(to_[:, :, :, at:at + D], z)
                    link(ins)
                    part = to_[:, :, :, slots[0]:slots[0] + D]
                    if slots is first_slots:
                        link(pool.tensor_tensor(z, z, part, ALU.subtract))
                return pool.tensor_tensor(to_[:, :, :, third_slot:third_slot + D], z, part, ALU.subtract)

            def stack_q(i):
                pool.wait_ge(qv_taken, 2 * i + 1)
                link(rotate(qraw[:, i], i, 0))
                split(qraw[:, i], qn[:, i * TPC:(i + 1) * TPC], (0, 8, S_C), (16, 24), S_C + 8).then_inc(q_split, 1)

            def stack_k(i):
                pool.wait_ge(k_taken, i + 1)
                if i > DVE_K:
                    pool.wait_ge(split_s, i)
                z = kraw_pool[:, i - DVE_K]
                link(rotate(z, i, 1))
                pool.wait_ge(split_s, i)
                split(z, kn[:, i * TPC:(i + 1) * TPC], (0,), (8,), S_C).then_inc(split_s, 1)

            pool.wait_ge(w1_s, 16)
            pool.wait_ge(k_s, 16)
            pool.memset(qa[:, 1, :, :].bitcast(F32), 0.0).then_inc(pads_s, 1)
            sides = vt[:, :, :, :].rearrange("p t (a b h) s -> p (t a) b h s", a=2, b=2)
            pool.memset(sides[:, :, 0, :, D:], 0.0)
            pool.memset(sides[:, :, 1, :, 0:16], 0.0)
            link(pool.memset(sides[:, :, 1, :, 16 + D:], 0.0))
            for b in range(2):
                pool.memset(sides[:, :, b, :, 16 * b + D:16 * b + D + 1], 1.0)
            for i in range(DVE_K, CHUNKS):
                stack_k(i)
            for i in range(CHUNKS):
                pool.wait_ge(qv_taken, 2 * i + 2)
                for g in range(QUADS):
                    at = 16 * (g % 2)
                    v = vt[:, i * TPC:(i + 1) * TPC, HQ * g:HQ * g + HQ, at:at + D]
                    bias = wcol("qkv_b", 2 * C + 32 * g, 2 * C + 32 * g + 32).rearrange("p (h d) -> p h d", h=HQ)
                    ins = pool.tensor_tensor(v, v, bias.unsqueeze(1).broadcast_to([P, TPC, HQ, D]), ALU.add)
                ins.then_inc(values_s, 1)
            for i in range(1, CHUNKS):
                pool.wait_ge(q_split, i)
                if i == 1:
                    pool.wait_ge(split_s, CHUNKS)
                stack_q(i)
            pool.wait_ge(w2_s, 16)
            pool.wait_ge(xn_s, CHUNKS)
            pb = wcol("proj_b").unsqueeze(1).broadcast_to([P, NT, C])
            pool.tensor_tensor(x[:, :, :], x[:, :, :], pb, ALU.add).then_inc(xb_s, 1)
            for q in range(CHUNKS, 3 * CHUNKS):
                root(q)
            pool.wait_ge(xn_s, 3 * CHUNKS)
            pb = wcol("lin_proj_b").unsqueeze(1).broadcast_to([P, NT, C])
            pool.tensor_tensor(x[:, :, :], x[:, :, :], pb, ALU.add).then_inc(xb_s, 1)
            for q in range(3 * CHUNKS, 4 * CHUNKS):
                root(q)

        @block.scalar
        def _(act):
            def store_ht(q, dst, bank=B_OUT):
                act.wait_ge(xt_s, q + 1)
                act.activation(dst, ps[:, bank, :], ACT.Copy).then_inc(ht_s, 1)

            def apply_norm(q):
                i = NORMS[q][1]
                act.wait_ge(rstd_s, q + 1)
                if q >= 2:
                    act.wait_ge(xt_s, q - 1)
                for t in range(TPC):
                    ins = act.activation(xn[:, q % 2, t, :], x[:, i * TPC + t, :], ACT.Identity,
                                         bias=shift[:, q % CHUNKS, t:t + 1], scale=rstd[:, q % CHUNKS, t:t + 1])
                ins.then_inc(xn_s, 1)

            def store_k(i):
                act.wait_ge(k_mm, i + 1)
                act.activation(kraw_pool[:, i - DVE_K], ps[:, B_K, :].rearrange("p (t c) -> p t c", t=TPC),
                               ACT.Copy).then_inc(k_taken, 1)

            def store_qv(i):
                act.wait_ge(qv_mm, 2 * i + 1)
                act.activation(qraw[:, i], ps[:, B_Q, :].rearrange("p (t c) -> p t c", t=TPC),
                               ACT.Copy).then_inc(qv_taken, 1)
                act.wait_ge(qv_mm, 2 * i + 2)
                to = vt[:, i * TPC:(i + 1) * TPC, :, :].rearrange("p t (a b h) s -> p (t a) b h s", a=2, b=2)
                of = ps[:, B_V, :].rearrange("p (t b h d) -> p t b h d", b=2, h=HQ, d=D)
                for b in range(2):
                    ins = act.activation(to[:, :, b, :, 16 * b:16 * b + D], of[:, :, b], ACT.Copy)
                ins.then_inc(qv_taken, 1)

            def repeats(i):
                act.wait_ge(split_s, i + 1)
                t = slice(i * TPC, (i + 1) * TPC)
                k = kn[:, t, :, :]
                for to, of in ((16, 0), (24, 8), (S_C + 8, 0)):
                    last = act.activation(k[:, :, :, to:to + D], k[:, :, :, of:of + D], ACT.Copy)
                last.then_inc(dups_s, 1)

            def keys_of(bank, g, i):
                src = ps[:, bank, :].bitcast(BF16).rearrange("p (a n) -> p a n", a=2)
                return act.activation(kb[:, 2 * g:2 * g + 2, i * CW:(i + 1) * CW], src, ACT.Copy)

            def first_keys(i):
                act.wait_ge(kt_s, i + 1)
                keys_of(B_OUT, 0, i).then_inc(kt_used, 1)

            def first_queries():
                act.wait_ge(q0t_s, 1)
                act.wait_ge(pads_s, 2)
                src = ps[:, B_PAIR, :].bitcast(BF16).rearrange("p (a n) -> p a n", a=2)
                for odd in range(2):
                    rows = slice(SL * odd, SL * odd + SL)
                    last = act.activation(qa[rows, 0, odd:HQ:2, :], src[rows], ACT.Copy)
                last.then_inc(q0_s, 1)

            def first_ht(i):
                store_ht(i, ht0[:, 1 + i * CW:1 + (i + 1) * CW], B_XT + i % 2)

            apply_norm(0)
            apply_norm(1)
            first_ht(0)
            apply_norm(2)
            store_qv(0)
            first_ht(1)
            apply_norm(3)
            store_qv(1)
            first_ht(2)
            first_ht(3)
            repeats(0)
            first_keys(0)
            first_queries()
            act.wait_ge(k_taken, DVE_K)
            store_k(2)
            store_qv(2)
            repeats(1)
            first_keys(1)
            store_k(3)
            store_qv(3)
            repeats(2)
            first_keys(2)

            def store_queries(part, n, a):
                act.wait_ge(ring_s, part.ring(("queries", n, a)))
                src = ps[:, part.bank(("queries", n, a)), 0:CW // 2].bitcast(BF16)
                for odd in range(2):
                    rows = slice(SL * odd, SL * odd + SL)
                    last = act.activation(qa[rows, n % 2, 2 * a + odd, :], src[rows, :], ACT.Copy)
                last.then_inc(ring_used, 1)

            def store_stack(part, n, a):
                act.wait_ge(ring_s, part.ring(("stack", n, a)))
                src = ps[:, part.bank(("stack", n, a)), 0:CW // 2].bitcast(BF16)
                act.activation(qb[:, n % 2, a, :], src, ACT.Copy).then_inc(ring_used, 1)

            def store_beside(part, key):
                what, n = key[:2]
                if what == "queries":
                    store_queries(part, n, key[2])
                elif what == "stack":
                    store_stack(part, n, key[2])
                else:
                    act.wait_ge(ring_s, part.ring(key))
                    bank = ps[:, part.bank(key), :]
                    if what == "sums":
                        ins = act.activation(turned, bank, ACT.Copy)
                    elif what == "att":
                        ins = act.activation(attT, bank, ACT.Copy)
                    else:
                        ins = act.activation(proj, bank, ACT.Copy)
                    ins.then_inc(ring_used, 1)

            def store_sums(part, m):
                act.wait_ge(pv_s, part.unit(2 * m + 1, STEPS, STEPS))
                act.activation(ot[:, m % 2, :], ps[:, B_OUT, :], ACT.Copy).then_inc(ot_s, 1)

            def step(part, n, kt):
                for h in range(HQ):
                    key = ("scores", n, kt, h)
                    act.wait_ge(ring_s, part.ring(key))
                    j = (n * STEPS + kt) * HQ + h
                    if h == 0 and n * STEPS + kt >= PROBS // HQ:
                        act.wait_ge(pv_s, part.unit(n, STEPS, kt - PROBS // HQ + 1))
                    act.activation(probs[:, j % PROBS, :], ps[:, part.bank(key), :], ACT.Exp,
                                   scale=SCALE).then_inc(ring_used, 1)
                if kt == 0 and n >= 1 and n % 2 == 0:
                    store_sums(part, n // 2 - 1)
                for key in beside(n, kt):
                    store_beside(part, key)
                if n >= UNITS - 2:
                    for job, i in LATE_ACT.get((n - UNITS + 1) * STEPS + kt, ()):
                        if job == "gate":
                            gate_r(i)
                        else:
                            late_ht(1 if job == "ht" else 2, i)

            def late_ht(norm, i):
                dst = ht0 if norm == 2 else ht1
                store_ht(NORMS.index((norm, i)), dst[:, 1 + i * CW:1 + (i + 1) * CW], B_OUT if norm == 3 else B_HT)

            def gate_r(i):
                act.wait_ge(r_s, i + 1)
                if i >= 2:
                    act.wait_ge(xf_s, i - 1)
                act.activation(sg[:, i % 2, :], ps[:, B_R, :], ACT.Tanh, scale=0.5).then_inc(sg_s, 1)

            start = before()
            act.wait_ge(pads_s, 3)
            for key in start_keys:
                if key == start_keys[EARLY]:
                    repeats(CHUNKS - 1)
                    first_keys(CHUNKS - 1)
                if key[0] == "keys":
                    act.wait_ge(ring_s, start.ring(key))
                    keys_of(start.bank(key), *key[1:]).then_inc(ring_used, 1)
                elif key[0] == "queries":
                    store_queries(start, *key[1:])
                else:
                    store_stack(start, *key[1:])
            end = attention(act, step)
            store_sums(end, UNITS // 2 - 1)
            store_beside(end, LAST_ITEM)

            late_ht(1, CHUNKS - 1)
            gate_r(CHUNKS - 1)
            late_ht(2, CHUNKS - 1)

            def ffn(i):
                q = CHUNKS + i
                act.wait_ge(kk_s, q + 1)
                if i >= 1:
                    act.wait_ge(ks_s, q)
                act.activation(kr, ps[:, 1 + 3 * (i % 2), :], ACT.Relu).then_inc(kr_s, 1)
                act.wait_ge(kr_s, i + 1)
                act.wait_ge(v_s, q - 1)
                act.activation(ks[:, i % 2, :], kr, ACT.Square).then_inc(ks_s, 1)
                act.wait_ge(r_s, q + 1)
                act.wait_ge(xf_s, q - 1)
                act.activation(sg[:, i % 2, :], ps[:, 3 * (i % 2), :], ACT.Tanh, scale=0.5).then_inc(sg_s, 1)

            def store_att3(i):
                act.wait_ge(lt_s, i + 1)
                act.activation(att3[:, i % 2, :], ps[:, 4 + i % 2, :], ACT.Copy).then_inc(lta_s, 1)

            def last_norm(i):
                apply_norm(NORMS.index((3, i)))

            store_att3(0)
            store_att3(1)
            last_norm(0)
            store_att3(2)
            late_ht(3, 0)
            last_norm(1)
            store_att3(3)
            late_ht(3, 1)
            ffn(0)
            last_norm(2)
            ffn(1)
            late_ht(3, 2)
            last_norm(3)
            late_ht(3, 3)
            ffn(2)
            ffn(3)

        @block.tensor
        def _(pe):
            pe.wait_ge(k_s, 16)
            pe.wait_ge(identb_s, 1)

            def turn_xn(q, bank=B_OUT, free=None):
                pe.wait_ge(xn_s, q + 1)
                free = q if free is None else free
                if free > 0:
                    pe.wait_ge(ht_s, free)
                for t in range(TPC):
                    last = pe.transpose(ps[:, bank, t * P:(t + 1) * P], xn[:, q % 2, t, :], ident)
                last.then_inc(xt_s, 1)

            def qkv(i, part):
                if part == 0:
                    pe.wait_ge(ht_s, i + 1)
                    if i == 0:
                        pe.wait_ge(w1_s, 16)
                bank, m, free, ready = ((B_K, 1, k_taken, k_mm), (B_Q, 0, qv_taken, qv_mm),
                                        (B_V, 2, qv_taken, qv_mm))[part]
                if i >= 1:
                    pe.wait_ge(free, i if part == 0 else 2 * i - 2 + part)
                for t in range(TPC):
                    tile = i * TPC + t
                    last = pe.matmul(ps[:, bank, t * C:(t + 1) * C], ht0[:, 1 + tile * P:1 + (tile + 1) * P],
                                     wcol("qkv", m * C, (m + 1) * C), start=True, stop=True)
                last.then_inc(ready, 1)

            def turn_keys(bank, g, i):
                dst = ps[:, bank, :].bitcast(BF16)
                for a in range(2):
                    for t in range(TPC):
                        src = kn_rows[:, i * TPC + t, 2 * SL * (2 * g + a):2 * SL * (2 * g + a + 1)]
                        at = a * CW + t * P
                        last = pe.transpose(dst[:, at:at + P], src, identb[:, :])
                return last

            def first_keys(i):
                pe.wait_ge(dups_s, i + 1)
                if i == 0:
                    pe.wait_ge(pads_s, 1)
                else:
                    pe.wait_ge(kt_used, i)
                turn_keys(B_OUT, 0, i).then_inc(kt_s, 1)

            def first_queries():
                pe.wait_ge(q_split, 1)
                dst = ps[:, B_PAIR, :].bitcast(BF16)
                for a in range(2):
                    for t in range(TPC):
                        at = a * CW + t * P
                        last = pe.transpose(dst[:, at:at + P], qn_rows[:, t, 2 * SL * a:2 * SL * (a + 1)], identb[:, :])
                last.then_inc(q0t_s, 1)

            def first_turn(i):
                turn_xn(i, B_XT + i % 2, i - 1)

            for i in range(2):
                first_turn(i)
                for part in range(3):
                    qkv(i, part)
            first_turn(2)
            first_turn(3)
            first_keys(0)
            first_queries()
            for part in range(3):
                qkv(2, part)

            def turn_q(part, key):
                _, n, a = key
                free = part.ring(key, 1 - SCORE_BANKS)
                if not isinstance(free, int) or free > 0:
                    pe.wait_ge(ring_used, free)
                if key[0] == "queries":
                    pe.wait_ge(q_split, part.c + (n // QUADS + 1))
                pe.sem_inc(turns_begun, 1)
                dst = ps[:, part.bank(key), :].bitcast(BF16)
                h = SL * (HQ * (n % QUADS) + 2 * a)
                for t in range(TPC):
                    rows = qn_rows[:, bass.ds(part.chunk_tile(n, t), 1), :].rearrange("p a s -> p (a s)")
                    last = pe.transpose(dst[:, t * P:(t + 1) * P], rows[:, h:h + 2 * SL], identb[:, :])
                last.then_inc(ring_s, 1)

            def max_scores(part, n, s, pr):
                j, t = divmod(s, TPC)
                if not (isinstance(part.unit(n), int) and n == 0 and s == 0):
                    pe.wait_ge(pair_used, part.unit(n, 2 * STEPS, 2 * s - 1 + pr))
                for a in range(2):
                    last = pe.matmul(ps[:, B_PAIR + 2 * pr + a, :], qa[:, n % 2, 2 * pr + a, t * P:(t + 1) * P],
                                     kb[:, 2 * (n % QUADS) + pr, j * CW:(j + 1) * CW], start=True, stop=True)
                last.then_inc(pair_s, 1)

            def sums(part, n, kt):
                g = n % QUADS
                if kt == 0 and n >= 1 and n % 2 == 0:
                    pe.wait_ge(ot_s, part.pair(n // 2))
                pe.wait_ge(ring_used, part.ring(("scores", n, kt, HQ - 1)))
                for h in range(HQ):
                    j = (n * STEPS + kt) * HQ + h
                    last = pe.matmul(ps[32 * h:32 * h + 32, B_OUT, :], vt[:, kt, HQ * g + h, :],
                                     probs[:, j % PROBS, :], start=(kt == 0 and n % 2 == 0),
                                     stop=(kt == STEPS - 1 and n % 2 == 1))
                last.then_inc(pv_s, 1)

            def ring_free(part, key):
                pe.wait_ge(ring_used, part.ring(key, 1 - SCORE_BANKS))

            def turn_sums(part, m):
                key = ("sums", m)
                pe.wait_ge(ot_s, part.pair(m + 1))
                ring_free(part, key)
                for t in range(TPC):
                    last = pe.transpose(ps[:, part.bank(key), t * P:(t + 1) * P], ot[:, m % 2, t * P:(t + 1) * P], ident)
                last.then_inc(ring_s, 1)

            def turn_attn(part, key):
                n = key[1]
                pe.wait_ge(attn_s, part.pair(n // 2))
                ring_free(part, key)
                for t in range(TPC):
                    last = pe.transpose(ps[:, part.bank(key), t * P:(t + 1) * P], attn[:, t, :], ident)
                last.then_inc(ring_s, 1)

            def project(part, key):
                pe.wait_ge(ring_used, part.ring(("att", key[1])))
                ring_free(part, key)
                for t in range(TPC):
                    last = pe.matmul(ps[:, part.bank(key), t * P:(t + 1) * P], attT[:, t * P:(t + 1) * P],
                                     wcol("proj"), start=True, stop=True)
                last.then_inc(ring_s, 1)

            def do_beside(part, key):
                what, n = key[:2]
                if what == "sums":
                    turn_sums(part, n)
                elif what == "att":
                    turn_attn(part, key)
                elif what == "proj":
                    project(part, key)
                else:
                    if what == "stack":
                        pe.wait_ge(max_s, part.unit(n, 1, 1))
                    turn_q(part, key)

            def step(part, n, kt):
                a = part.a_step(n, kt)

                def maximum(pr):
                    if a is None:
                        return
                    if pr == 0:
                        if a[1] == 0:
                            key = ("queries", a[0], 1)
                            pe.wait_ge(ring_used, part.ring(key) if key in part.items else before().ring(key))
                    max_scores(part, *a, pr)

                def scores(heads):
                    for h in heads:
                        key = ("scores", n, kt, h)
                        pe.wait_ge(ring_used, part.ring(key, 1 - SCORE_BANKS))
                        rows = slice(SL * (h % 2), SL * (h % 2) + SL)
                        pe.matmul(ps[:, part.bank(key), :], kb[rows, 2 * (n % QUADS) + h // 2, kt * P:(kt + 1) * P],
                                  qb[rows, n % 2, h // 2, :], start=True, stop=True).then_inc(ring_s, 1)

                maximum(0)
                scores((0, 1))
                maximum(1)
                scores((2,))
                if kt >= 1:
                    sums(part, n, kt - 1)
                elif n > part.first:
                    sums(part, n - 1, STEPS - 1)
                elif n >= 1:
                    carried_sums(part, n)
                scores((3,))
                for key in beside(n, kt):
                    do_beside(part, key)
                if n >= UNITS - 2:
                    for job in LATE_PE.get((n - UNITS + 1) * STEPS + kt, ()):
                        late_job(*job)

            def natural(bank, groups, width=P):
                for t in range(TPC):
                    for m, (z, at, wt) in enumerate(groups):
                        last = pe.matmul(ps[:, bank, t * width:(t + 1) * width], z[:, at + t * P:at + (t + 1) * P],
                                         wt, start=(m == 0), stop=(m == len(groups) - 1))
                return last

            def products_rk(q, i, r_bank, k_bank):
                pe.wait_ge(mix_s, 2 * q + 1)
                pe.matmul(ps[:, k_bank, :], wcol("k"), xk[:, i % 2, :], start=True, stop=True).then_inc(kk_s, 1)
                pe.wait_ge(mix_s, 2 * q + 2)
                natural(r_bank, ((xr[:, i % 2, :], 0, wcol("r")),)).then_inc(r_s, 1)

            def late_job(job, i):
                if job == "ht":
                    if i == 0:
                        pe.wait_ge(pair_used, 2 * UNITS * STEPS)
                    elif i == CHUNKS - 1:
                        pe.wait_ge(q3a_s, 2)
                    turn_xn(NORMS.index((1, i)), B_HT)
                elif job == "rk":
                    if i >= 1:
                        pe.wait_ge(sg_s, i)
                        pe.wait_ge(xf_s, i)
                    if i == CHUNKS - 1:
                        pe.wait_ge(kv3a_s, 2)
                    products_rk(i, i, B_R, B_KV)
                elif job == "v":
                    pe.wait_ge(ks_s, i + 1)
                    natural(B_KV, ((ks[:, i % 2, :], 0, wcol("v")),)).then_inc(v_s, 1)
                elif job == "ht3":
                    if i >= 1:
                        pe.wait_ge(q3a_s, 3 if i == CHUNKS - 1 else 1)
                    turn_xn(NORMS.index((2, i)), B_HT)
                elif job == "qkv3":
                    ffns = CHUNKS if i >= CHUNKS - 2 else CHUNKS - 1
                    pe.wait_ge(ht_s, NORMS.index(((2, 0), (2, 2), (1, 3), (2, 3))[i]) + 1)
                    at = 1 + i * CW
                    for what in QKV3[i]:
                        if what == "q":
                            pe.matmul(ps[:, B_HT, :], wcol("lin_qkv", 0, C), ht0[:, at:at + CW], start=True,
                                      stop=True).then_inc(q3_s, 1)
                            continue
                        if what == "k":
                            if i >= 1:
                                pe.wait_ge(kv3a_s, i)
                            pe.wait_ge(sg_s, ffns)
                        else:
                            pe.wait_ge(xf_s, ffns)
                        m, bank = (1, B_R) if what == "k" else (2, B_KV)
                        natural(bank, ((ht0, at, wcol("lin_qkv", m * C, (m + 1) * C)),)).then_inc(kv3_s, 1)
                else:
                    pe.wait_ge(kv3a_s, i + 1)
                    for t in range(TPC):
                        last = pe.matmul(ps[:, B_CTX, 0:C + 1], kn3[:, i % 2, t, :], vn3[:, i % 2, t, 0:C + 1],
                                         start=(i == 0 and t == 0), stop=(i == CHUNKS - 1 and t == TPC - 1))
                    last.then_inc(ctx_s, 1)

            def carried_sums(part, n):
                g = (n - 1) % QUADS
                pe.wait_ge(ring_used, part.ring(("scores", n, 0, 0), 0))
                for h in range(HQ):
                    j = ((n - 1) * STEPS + STEPS - 1) * HQ + h
                    last = pe.matmul(ps[32 * h:32 * h + 32, B_OUT, :], vt[:, STEPS - 1, HQ * g + h, :],
                                     probs[:, j % PROBS, :], start=False, stop=False)
                last.then_inc(pv_s, 1)

            start = before()
            items = iter(start_keys)

            def turn_next():
                key = next(items)
                if key[0] != "keys":
                    turn_q(start, key)
                    return
                free = start.ring(key, 1 - SCORE_BANKS)
                if free > 0:
                    pe.wait_ge(ring_used, free)
                turn_keys(start.bank(key), *key[1:]).then_inc(ring_s, 1)

            pe.wait_ge(q0_s, 1)
            pe.wait_ge(ht_s, CHUNKS)
            KEYS_AT = (0, 5, 11)
            for s in range(LEAD):
                if s < STEPS and s % TPC == 0:
                    pe.wait_ge(kt_used, s // TPC + 1)
                if s == STEPS:
                    pe.wait_ge(ring_used, start.ring(("queries", 1, 1)))
                for pr in range(2):
                    max_scores(start, s // STEPS, s % STEPS, pr)
                if s in KEYS_AT:
                    first_keys(1 + KEYS_AT.index(s))
                if 1 <= s <= 3:
                    qkv(3, s - 1)
                if s == KEYS_AT[1]:
                    pe.wait_ge(k_taken, CHUNKS)
                    pe.wait_ge(qv_taken, 2 * CHUNKS)
                if KEYS_AT[1] <= s < STEPS:
                    turn_next()
                    if s < KEYS_AT[1] + EARLY - (KEYS_AT[2] - KEYS_AT[1]):
                        turn_next()
                elif s == LEAD - 2:
                    pe.wait_ge(max_s, 1)
                    for a in range(2):
                        turn_next()
            pe.wait_ge(values_s, CHUNKS)
            pe.wait_ge(w2_s, 16)
            pe.wait_ge(ring_used, RING0)
            end = attention(pe, step)
            sums(end, UNITS - 1, STEPS - 1)
            pe.wait_ge(ot_s, UNITS // 2)
            for t in range(TPC):
                last = pe.transpose(ps[:, B_OUT, t * P:(t + 1) * P], ot[:, (UNITS // 2 - 1) % 2, t * P:(t + 1) * P], ident)
            last.then_inc(last_s, 1)
            do_beside(end, LAST_ITEM)
            pe.wait_ge(ring_used, end.ring(LAST_ITEM))
            for t in range(TPC):
                last = pe.matmul(ps[:, B_OUT, t * P:(t + 1) * P], attT[:, t * P:(t + 1) * P], wcol("proj"),
                                 start=True, stop=True)
            last.then_inc(last_s, 1)
            for job, i in (("qkv3", 1), ("ctx", 0), ("ht", 3), ("ctx", 1), ("rk", 3), ("v", 3), ("qkv3", 2),
                           ("ht3", 3), ("ctx", 2), ("qkv3", 3), ("ctx", 3)):
                late_job(job, i)

            def ffn_rk(i):
                q = CHUNKS + i
                b = 3 * (i % 2)
                if i >= 2:
                    pe.wait_ge(sg_s, q - 1)
                    pe.wait_ge(ks_s, q - 1)
                products_rk(q, i, b, b + 1)

            def ffn_v(i):
                q = CHUNKS + i
                pe.wait_ge(ks_s, q + 1)
                pe.wait_ge(xf_s, q - 1)
                natural(2 + 3 * (i % 2), ((ks[:, i % 2, :], 0, wcol("v")),)).then_inc(v_s, 1)

            pe.wait_ge(ctxm_s, 1)

            def lin_out(i):
                if i >= 2:
                    pe.wait_ge(ln_s, i - 1)
                for t in range(TPC):
                    last = pe.matmul(ps[:, 2 * (i % 2) + t // 2, (t % 2) * 256:(t % 2) * 256 + C + H],
                                     qt[:, i * CW + t * P:i * CW + (t + 1) * P], ctxm, start=True, stop=True)
                last.then_inc(lo_s, 1)

            def lin_turn(i):
                pe.wait_ge(ln_s, i + 1)
                if i >= 2:
                    pe.wait_ge(lta_s, i - 1)
                for t in range(TPC):
                    last = pe.transpose(ps[:, 4 + i % 2, t * P:(t + 1) * P], at3[:, i % 2, t, :], ident)
                last.then_inc(lt_s, 1)

            def lin_proj(i):
                pe.wait_ge(lta_s, i + 1)
                if i >= 1:
                    pe.wait_ge(lx_s, i)
                natural(6, ((att3[:, i % 2, :], 0, wcol("lin_proj")),)).then_inc(lp_s, 1)

            def turn_last(i):
                turn_xn(NORMS.index((3, i)))

            lin_out(0)
            lin_out(1)
            lin_turn(0)
            lin_proj(0)
            for i in range(1, CHUNKS - 1):
                lin_turn(i)
                lin_out(i + 1)
                lin_proj(i)
            turn_last(0)
            lin_turn(CHUNKS - 1)
            turn_last(1)
            ffn_rk(0)
            lin_proj(CHUNKS - 1)
            ffn_v(0)
            ffn_rk(1)
            turn_last(2)
            ffn_v(1)
            turn_last(3)
            ffn_rk(2)
            ffn_rk(3)
            ffn_v(2)
            ffn_v(3)

        @block.vector
        def _(dve):
            links = [0]

            def link(ins):
                links[0] += 1
                ins.then_inc(chain, 1)
                dve.wait_ge(chain, links[0])

            dve.wait_ge(k_s, 16)
            dve.tensor_copy(identb[:, :], ident).then_inc(identb_s, 1)

            late_links = [0]

            def late_link(ins):
                late_links[0] += 1
                ins.then_inc(late_chain, 1)
                dve.wait_ge(late_chain, late_links[0])

            def ln_stats(q, i, link=link):
                if q >= 1:
                    dve.wait_ge(stats_s, q)
                if q >= CHUNKS:
                    dve.wait_ge(xn_s, q - CHUNKS + 1)
                for t in range(TPC):
                    ins = dve.bn_stats(stats[:, t, :], x[:, i * TPC + t, :])
                link(ins)
                for t in range(TPC):
                    ins = dve.bn_aggr(mv[:, q % CHUNKS, t, :], stats[:, t, :])
                ins.then_inc(stats_s, 1)

            def ln_apply(q, i):
                dve.wait_ge(rstd_s, q + 1)
                dve.wait_ge(stats_s, q + 1)
                if q >= 2:
                    dve.wait_ge(xt_s, q - 1)
                for t in range(TPC):
                    ins = dve.tensor_scalar(xn[:, q % 2, t, :], x[:, i * TPC + t, :], mv[:, q % CHUNKS, t, 0:1],
                                            rstd[:, q % CHUNKS, t:t + 1], ALU.subtract, ALU.mult)
                ins.then_inc(xn_s, 1)

            def stack_k(i):
                dve.wait_ge(k_mm, i + 1)
                dve.wait_ge(w1_s, 16)
                if i >= 1:
                    dve.wait_ge(q_split, 1)
                bias = wcol("qkv_b", C, 2 * C).unsqueeze(1).broadcast_to([P, TPC, C])
                dve.tensor_tensor(kraw, ps[:, B_K, :].rearrange("p (t c) -> p t c", t=TPC), bias,
                                  ALU.add).then_inc(k_taken, 1)
                dve.wait_ge(k_taken, i + 1)
                rotate(kraw, i)
                split(kn[:, i * TPC:(i + 1) * TPC], (0,), (8,), S_C).then_inc(split_s, 1)

            def stack_first_q():
                dve.wait_ge(qv_taken, 1)
                dve.wait_ge(split_s, 1)
                dve.wait_ge(pads_s, 2)
                q = qraw[:, 0]
                bias = wcol("qkv_b", 0, C).unsqueeze(1).broadcast_to([P, TPC, C])
                link(dve.tensor_tensor(q, q, bias, ALU.add))
                rotate(q, 0)
                split(qn[:, 0:TPC], (0, 8, S_C), (16, 24), S_C + 8).then_inc(q_split, 1)

            def rotate(z, i):
                v = z.rearrange("p t (g j two) -> p t g j two", g=H, two=2)
                r = krot.rearrange("p t (g j two) -> p t g j two", g=H, two=2)
                e, od = v[:, :, :, :, 0], v[:, :, :, :, 1]
                m = ktmp.rearrange("p t (two g j) -> p t g j two", two=2, g=H)
                m0, m1 = m[:, :, :, :, 0], m[:, :, :, :, 1]
                tt = slice(i * TPC, (i + 1) * TPC)
                cs = cos[:, tt, :].unsqueeze(2).broadcast_to([P, TPC, H, D // 2])
                sn = sin[:, tt, :].unsqueeze(2).broadcast_to([P, TPC, H, D // 2])
                dve.tensor_tensor(m0, od, sn, ALU.mult)
                dve.tensor_tensor(m1, od, cs, ALU.mult)
                dve.tensor_tensor(r[:, :, :, :, 0], e, cs, ALU.mult)
                link(dve.tensor_tensor(r[:, :, :, :, 1], e, sn, ALU.mult))
                dve.tensor_tensor(r[:, :, :, :, 0], r[:, :, :, :, 0], m0, ALU.subtract)
                link(dve.tensor_tensor(r[:, :, :, :, 1], r[:, :, :, :, 1], m1, ALU.add))

            def split(to_, first_slots, second_slots, third_slot):
                z = krot.rearrange("p t (h d) -> p t h d", h=H)
                for slots in (first_slots, second_slots):
                    for at in slots:
                        ins = dve.tensor_copy(to_[:, :, :, at:at + D], z)
                    link(ins)
                    part = to_[:, :, :, slots[0]:slots[0] + D]
                    if slots is first_slots:
                        link(dve.tensor_tensor(z, z, part, ALU.subtract))
                return dve.tensor_tensor(to_[:, :, :, third_slot:third_slot + D], z, part, ALU.subtract)

            def take_x(i):
                dve.wait_ge(x_in_s[i], 16)
                ln_stats(i, i)

            for i in range(CHUNKS):
                take_x(i)
            stack_k(0)
            stack_first_q()
            for i in range(1, DVE_K):
                stack_k(i)

            def take_max(part, n, s):
                j, t = divmod(s, TPC)
                for pr in range(2):
                    dve.wait_ge(pair_s, part.unit(n, 2 * STEPS, 2 * s + pr + 1))
                    dve.tensor_reduce(mpart[:, n % 2, t, 2 * pr:2 * pr + 2, j],
                                      ps[:, B_PAIR + 2 * pr:B_PAIR + 2 * pr + 2, :],
                                      AX.X, ALU.max).then_inc(pair_used, 1)

            LINKS = 2 * QUADS + QUADS // 2

            def put_max(part, n):
                g = n % QUADS
                before_ = links[0] + 2 * n + max(n - 1, 0) // 2
                if part.per:
                    before_ = part.c * LINKS + before_
                dve.wait_ge(pair_used, part.unit(n, 2 * STEPS, 2 * STEPS))
                dve.tensor_reduce(negm[:, :, :], mpart[:, n % 2], AX.X, ALU.max, negate=True).then_inc(chain, 1)
                dve.wait_ge(chain, before_ + 1)
                tiles = bass.ds(part.chunk_tile(n, 0), TPC)
                slot = qn[:, tiles, HQ * g:HQ * g + HQ, S_MAX]
                dve.tensor_copy(slot, negm[:, :, :]).then_inc(chain, 1)
                dve.wait_ge(chain, before_ + 2)
                dve.tensor_tensor(qn[:, tiles, HQ * g:HQ * g + HQ, S_MAX + 1], negm[:, :, :], slot,
                                  ALU.subtract).then_inc(max_s, 1)

            def scale_sums(part, m):
                if m < UNITS // 2 - 1 or part.per:
                    dve.wait_ge(ring_used, part.ring(("sums", m)))
                    of = turned
                else:
                    dve.wait_ge(last_s, 1)
                    of = ps[:, B_OUT, :]
                v = of.rearrange("p (t h b s) -> p t h b s", t=TPC, h=HQ, b=2)
                dve.reciprocal(rsum[:, :, :, :], v[:, :, :, :, D]).then_inc(chain, 1)
                done = links[0] + 2 * min(2 * m + 3, UNITS) + m + 1
                dve.wait_ge(chain, part.c * LINKS + done if part.per else done)
                for b in range(2):
                    at = 32 * (2 * (m % 2) + b)
                    ins = dve.tensor_tensor(attn[:, :, at:at + 32].rearrange("p t (h d) -> p t h d", h=HQ),
                                            v[:, :, :, b, 0:D],
                                            rsum[:, :, :, b].unsqueeze(3).broadcast_to([P, TPC, HQ, D]), ALU.mult)
                ins.then_inc(attn_s, 1)

            def add_proj(part, n):
                if n < UNITS or part.per:
                    dve.wait_ge(ring_used, part.ring(("proj", n)))
                    of = proj
                else:
                    dve.wait_ge(last_s, 2)
                    of = ps[:, B_OUT, :]
                dve.wait_ge(xb_s, 1)
                tiles = x[:, bass.ds(part.chunk_tile(n, -TPC), TPC), :]
                dve.tensor_tensor(tiles, tiles, of.rearrange("p (t c) -> p t c", t=TPC), ALU.add).then_inc(x1_s, 1)

            def step(part, n, kt):
                a = part.a_step(n, kt)
                if a is not None:
                    take_max(part, *a)
                    if a[1] == STEPS - 1:
                        put_max(part, a[0])
                if kt == SUMS_STEP + 1 and n >= 1 and n % 2 == 0:
                    scale_sums(part, n // 2 - 1)
                if kt == PROJ_STEP + 1 and n >= 1 and n % QUADS == 0:
                    add_proj(part, n)
                if n >= UNITS - 2:
                    for job, i in LATE_DVE.get((n - UNITS + 1) * STEPS + kt, ()):
                        late_job(job, i)

            def late_constants():
                dve.wait_ge(q_split, CHUNKS)
                dve.wait_ge(ring_used, last_stack)
                dve.memset(ht1[:, 0:1], 0.0)
                dve.memset(vn3[:, :, :, C:C + 1], 1.0).then_inc(late_s, 1)
                dve.wait_ge(late_s, 1)

            def mix(q, i):
                dve.wait_ge(ht_s, NORMS.index((1 if q < CHUNKS else 3, i)) + 1)
                if q >= 1:
                    dve.wait_ge(mix_s, 2 * q)
                if q >= 2:
                    dve.wait_ge(r_s, q - 1)
                h, before_ = ht1[:, 1 + i * CW:1 + (i + 1) * CW], ht1[:, i * CW:(i + 1) * CW]
                late_link(dve.tensor_tensor(diff, h, before_, ALU.subtract))
                dve.scalar_tensor_tensor(xk[:, i % 2, :], diff, wcol("mu", 1, 2), before_, ALU.mult,
                                         ALU.add).then_inc(mix_s, 1)
                dve.scalar_tensor_tensor(xr[:, i % 2, :], diff, wcol("mu", 0, 1), before_, ALU.mult,
                                         ALU.add).then_inc(mix_s, 1)

            def gate_add(q, i, bank):
                t = slice(i * TPC, (i + 1) * TPC)
                dve.wait_ge(sg_s, q + 1)
                dve.wait_ge(v_s, q + 1)
                late_link(dve.scalar_tensor_tensor(vs, sg[:, i % 2, :], 1.0, ps[:, bank, :], ALU.add, ALU.mult))
                dve.scalar_tensor_tensor(x[:, t, :], vs.rearrange("p (t c) -> p t c", t=TPC), 0.5, x[:, t, :],
                                         ALU.mult, ALU.add).then_inc(xf_s, 1)
                dve.wait_ge(xf_s, q + 1)

            def late_job(job, i):
                if job == "constants":
                    late_constants()
                elif job == "stats":
                    ln_stats(i, NORMS[i][1], late_link)
                elif job == "apply":
                    ln_apply(i, NORMS[i][1])
                elif job == "mix":
                    mix(i, i)
                elif job == "square":
                    dve.wait_ge(kk_s, i + 1)
                    if i >= 2:
                        dve.wait_ge(v_s, i - 1)
                    late_link(dve.tensor_scalar(kr, ps[:, B_KV, :], 0.0, None, ALU.max))
                    dve.tensor_tensor(ks[:, i % 2, :], kr, kr, ALU.mult).then_inc(ks_s, 1)
                elif job == "add":
                    gate_add(i, i, B_KV)
                else:
                    if i >= 2:
                        dve.wait_ge(ctx_s, i - 1)
                    for what in QKV3[i]:
                        if what == "q":
                            dve.wait_ge(q3_s, i + 1)
                            dve.tensor_scalar(qt[:, i * CW:(i + 1) * CW], ps[:, B_HT, :], 0.0, None,
                                              ALU.max).then_inc(q3a_s, 1)
                        elif what == "k":
                            dve.wait_ge(kv3_s, 2 * i + 1)
                            dve.tensor_scalar(kn3[:, i % 2, :, :], ps[:, B_R, :].rearrange("p (t c) -> p t c", t=TPC),
                                              0.0, None, ALU.max)
                        else:
                            dve.wait_ge(kv3_s, 2 * i + 2)
                            dve.tensor_copy(vn3[:, i % 2, :, 0:C],
                                            ps[:, B_KV, :].rearrange("p (t c) -> p t c", t=TPC)).then_inc(kv3a_s, 1)

            last_stack = last_part().ring(("stack", UNITS - 1, 1))
            start = before()
            for s in range(LEAD):
                take_max(start, s // STEPS, s % STEPS)
                if s % STEPS == STEPS - 1:
                    put_max(start, s // STEPS)
            end = attention(dve, step)
            scale_sums(end, UNITS // 2 - 1)
            add_proj(end, UNITS)
            dve.wait_ge(x1_s, CHUNKS)

            q = NORMS.index((1, CHUNKS - 1))
            ln_stats(q, CHUNKS - 1, late_link)
            late_job("qkv3", 1)
            ln_apply(q, CHUNKS - 1)
            for job in ("mix", "square", "add"):
                late_job(job, CHUNKS - 1)
            q = NORMS.index((2, CHUNKS - 1))
            ln_stats(q, CHUNKS - 1, late_link)
            late_job("qkv3", 2)
            ln_apply(q, CHUNKS - 1)
            late_job("qkv3", CHUNKS - 1)
            dve.wait_ge(ctx_s, CHUNKS)
            dve.tensor_tensor(ctxm[:, 0:C], block_mask, ps[:, B_CTX, 0:C], ALU.mult)
            late_link(dve.tensor_copy(ksum, ps[:, B_CTX, C:C + 1]))
            heads = block_mask.rearrange("p (h d) -> p h d", h=H)[:, :, 0]
            dve.tensor_scalar(ctxm[:, C:C + H], heads, ksum, None, ALU.mult).then_inc(ctxm_s, 1)

            def lin_scale(i):
                dve.wait_ge(lo_s, i + 1)
                if i >= 2:
                    dve.wait_ge(lt_s, i - 1)
                if i >= 1:
                    dve.wait_ge(ln_s, i)
                v = ps[:, 2 * (i % 2):2 * (i % 2) + 2, :].rearrange("p b (t c) -> p (b t) c", t=2)
                late_link(dve.tensor_scalar(zz[:, 0], v[:, :, C:C + H], Z_EPS, None, ALU.add))
                late_link(dve.reciprocal(zz[:, 1], zz[:, 0]))
                dve.tensor_tensor(at3[:, i % 2].rearrange("p t (h d) -> p t h d", h=H),
                                  v[:, :, 0:C].rearrange("p t (h d) -> p t h d", h=H),
                                  zz[:, 1].unsqueeze(3).broadcast_to([P, TPC, H, D]), ALU.mult).then_inc(ln_s, 1)

            def lin_add(i):
                t = slice(i * TPC, (i + 1) * TPC)
                dve.wait_ge(lp_s, i + 1)
                if i == 0:
                    dve.wait_ge(xb_s, 2)
                dve.tensor_tensor(x[:, t, :], x[:, t, :], ps[:, 6, :].rearrange("p (t c) -> p t c", t=TPC),
                                  ALU.add).then_inc(lx_s, 1)
                dve.wait_ge(lx_s, i + 1)
                ln_stats(3 * CHUNKS + i, i, late_link)

            lin_scale(0)
            lin_scale(1)
            for i in range(CHUNKS):
                if i >= 2:
                    mix(CHUNKS + i - 2, i - 2)
                lin_add(i)
                if i + 2 < CHUNKS:
                    lin_scale(i + 2)
            for i in range(CHUNKS):
                gate_add(CHUNKS + i, i, 2 + 3 * (i % 2))
                if i + 2 < CHUNKS:
                    mix(CHUNKS + i + 2, i + 2)


def rope_tables():
    import numpy as np
    inv = (np.float32(1.0) / np.float32(10000.0) ** (np.arange(0, D, 2, dtype=np.float32) / np.float32(D))).astype(np.float32)
    freqs = (np.arange(N, dtype=np.float32)[:, None] * inv[None, :]).astype(np.float32)

    def lay(z):
        return z.astype(np.float32).reshape(NT, P, D // 2).transpose(1, 0, 2).reshape(P, NT * D // 2)
    return lay(np.cos(freqs.astype(np.float64))), lay(np.sin(freqs.astype(np.float64)))


def kernel(**inputs):
    import numpy as np
    import concourse.bacc as bacc
    from concourse.bass_utils import run_bass_kernel_spmd

    g = {k: np.asarray(v) for k, v in inputs.items()}

    def rows(v):
        return np.broadcast_to(v[None, :], (P, v.shape[0]))

    parts = {
        "qkv": g["L0_attn_a_qkv_w"].T, "qkv_b": rows(g["L0_attn_a_qkv_b"]), "proj": g["L0_attn_a_proj_w"].T,
        "proj_b": rows(g["L0_attn_a_proj_b"]), "lin_qkv": g["L0_attn_b_w_qkv"].T, "lin_proj": g["L0_attn_b_w_proj"].T,
        "lin_proj_b": rows(g["L0_attn_b_b_proj"]), "r": g["L0_ffn_W_r"].T, "k": g["L0_ffn_W_k"].T,
        "v": g["L0_ffn_W_v"].T, "mu": np.stack([g["L0_ffn_mu_r"], g["L0_ffn_mu_k"]], axis=1),
    }
    weights = np.ascontiguousarray(np.concatenate([parts[n] for n in W_COLS], axis=1))
    cos, sin = rope_tables()
    head = np.arange(P) // D
    consts = np.ascontiguousarray(np.concatenate(
        [cos, sin, np.eye(P, dtype=np.float32), (head[:, None] == head[None, :]).astype(np.float32)], axis=1))
    xs = np.ascontiguousarray(g["L0_attn_a_x"].reshape(N, C))

    nc = bacc.Bacc("TRN2", target_bir_lowering=False, num_devices=1)
    arrays = {"x_dram": xs, "w_dram": weights, "k_dram": consts}
    args = [nc.dram_tensor(n, a.shape, mybir.dt.from_np(a.dtype), kind="ExternalInput").ap() for n, a in arrays.items()]
    out = nc.dram_tensor("out_dram", (N, C), F32, kind="ExternalOutput").ap()
    build(nc, *args, out)
    r = run_bass_kernel_spmd(nc, [arrays], core_ids=[0])
    return r.results[0]["out_dram"].reshape(1, N, C)
```
